# Optimizing a Trainium2 kernel written in Bass

```python
import numpy as np
import jax
import jax.numpy as jnp

def _softmax(x, axis=-1):
    return jax.nn.softmax(x, axis=axis)

def _gelu(x):
    return jax.nn.gelu(x, approximate=True)

def _silu(x):
    return jax.nn.silu(x)

def _sigmoid(x):
    return jax.nn.sigmoid(x)

def _layernorm(x, axis=-1, eps=1e-05):
    m = jnp.mean(x, axis=axis, keepdims=True)
    v = jnp.var(x, axis=axis, keepdims=True)
    return (x - m) / jnp.sqrt(v + eps)

def _scatter_add(tgt, idx, src, axis=0):
    return tgt.at[idx].add(src)

def _segment_sum(src, seg, n):
    return jax.ops.segment_sum(src, seg, n)
kernel_name = 'mk_adaln_d1_jaxref_r8_e26deb'

def setup_inputs(seed: int=0):
    np.random.seed(seed)
    _w = jnp.asarray

    def _L0_attn_setup():
        import jax, jax.numpy as jnp
        import numpy as np
        DIM = 256
        HEADS = 16
        HEAD_DIM = DIM // HEADS
        KVC = 64
        QC = 128
        B, S = (2, 256)
        ROPE_BASE = 10000.0

        def apply_rope(x):
            b, s, h, d = x.shape
            half = d // 2
            inv_freq = 1.0 / ROPE_BASE ** (jnp.arange(0, d, 2, dtype=jnp.float32) / d)
            ang = jnp.arange(s, dtype=jnp.float32)[:, None] * inv_freq[None, :]
            cos = jnp.cos(ang)[None, :, None, :].astype(x.dtype)
            sin = jnp.sin(ang)[None, :, None, :].astype(x.dtype)
            xs = x.reshape(b, s, h, half, 2)
            x0, x1 = (xs[..., 0], xs[..., 1])
            r0 = x0 * cos - x1 * sin
            r1 = x1 * cos + x0 * sin
            return jnp.stack([r0, r1], axis=-1).reshape(b, s, h, d)
        key = jax.random.key(seed)
        ks = jax.random.split(key, 9)

        def w(k, shape):
            fan_in = shape[0]
            return jax.random.normal(k, shape, dtype=jnp.float32) / np.sqrt(fan_in)
        return {'x': jax.random.normal(ks[0], (B, S, DIM), dtype=jnp.float32), 'w_kv_down': w(ks[1], (DIM, KVC)), 'w_kv_up_k': w(ks[2], (KVC, HEADS * HEAD_DIM)), 'w_kv_up_v': w(ks[3], (KVC, HEADS * HEAD_DIM)), 'w_q_down': w(ks[4], (DIM, QC)), 'w_q_up': w(ks[5], (QC, HEADS * HEAD_DIM)), 'w_k_rope': w(ks[6], (DIM, HEAD_DIM)), 'w_q_rope': w(ks[7], (DIM, HEAD_DIM)), 'w_out': w(ks[8], (HEADS * HEAD_DIM, DIM))}
    _L0_attn_in = _L0_attn_setup()

    def _L0_ffn_setup():
        import jax, jax.numpy as jnp
        import numpy as np
        B, S, D, H = (4, 256, 256, 1024)

        def fwht(x):
            orig_shape = x.shape
            n = orig_shape[-1]
            x = x.reshape(-1, n)
            h = 1
            while h < n:
                xb = x.reshape(-1, n // (2 * h), 2, h)
                a = xb[:, :, 0, :]
                b = xb[:, :, 1, :]
                x = jnp.stack([a + b, a - b], axis=2).reshape(-1, n)
                h *= 2
            scale = jnp.asarray(1.0 / np.sqrt(n), dtype=x.dtype)
            return (x * scale).reshape(orig_shape)
        key = jax.random.key(seed)
        kx, k1, k2, k3 = jax.random.split(key, 4)
        x = jax.random.normal(kx, (B, S, D), dtype=jnp.float32)
        W1 = jax.random.normal(k1, (H, D), dtype=jnp.float32) * (1.0 / np.sqrt(D))
        W2 = jax.random.normal(k2, (D, H), dtype=jnp.float32) * (1.0 / np.sqrt(H))
        W3 = jax.random.normal(k3, (H, D), dtype=jnp.float32) * (1.0 / np.sqrt(D))
        return {'x': x, 'W1': W1, 'W2': W2, 'W3': W3}
    _L0_ffn_in = _L0_ffn_setup()
    _L0_c = _w((lambda *s: np.random.randn(*s).astype(np.float32) * 0.05)(8, 256))
    _L0_wmod = _w((lambda *s: np.random.randn(*s).astype(np.float32) * 0.05)(256, 6 * 256) * 256 ** (-0.5))
    _d = {'L0_attn_x': _L0_attn_in['x'], 'L0_attn_w_kv_down': _L0_attn_in['w_kv_down'], 'L0_attn_w_kv_up_k': _L0_attn_in['w_kv_up_k'], 'L0_attn_w_kv_up_v': _L0_attn_in['w_kv_up_v'], 'L0_attn_w_q_down': _L0_attn_in['w_q_down'], 'L0_attn_w_q_up': _L0_attn_in['w_q_up'], 'L0_attn_w_k_rope': _L0_attn_in['w_k_rope'], 'L0_attn_w_q_rope': _L0_attn_in['w_q_rope'], 'L0_attn_w_out': _L0_attn_in['w_out'], 'L0_ffn_W1': _L0_ffn_in['W1'], 'L0_ffn_W2': _L0_ffn_in['W2'], 'L0_ffn_W3': _L0_ffn_in['W3'], 'L0_c': _L0_c, 'L0_wmod': _L0_wmod}
    _x0 = _d['L0_attn_x']
    _d['L0_attn_x'] = jax.random.normal(jax.random.fold_in(jax.random.key(seed), 1), (8, 512, 256), dtype=_x0.dtype)
    del _x0
    return _d

def reference(L0_attn_x, L0_attn_w_kv_down, L0_attn_w_kv_up_k, L0_attn_w_kv_up_v, L0_attn_w_q_down, L0_attn_w_q_up, L0_attn_w_k_rope, L0_attn_w_q_rope, L0_attn_w_out, L0_ffn_W1, L0_ffn_W2, L0_ffn_W3, L0_c, L0_wmod):

    def _L0_attn_ref(x, w_kv_down, w_kv_up_k, w_kv_up_v, w_q_down, w_q_up, w_k_rope, w_q_rope, w_out):
        import jax, jax.numpy as jnp
        import numpy as np
        DIM = 256
        HEADS = 16
        HEAD_DIM = DIM // HEADS
        KVC = 64
        QC = 128
        B, S = (2, 256)
        ROPE_BASE = 10000.0

        def apply_rope(x):
            b, s, h, d = x.shape
            half = d // 2
            inv_freq = 1.0 / ROPE_BASE ** (jnp.arange(0, d, 2, dtype=jnp.float32) / d)
            ang = jnp.arange(s, dtype=jnp.float32)[:, None] * inv_freq[None, :]
            cos = jnp.cos(ang)[None, :, None, :].astype(x.dtype)
            sin = jnp.sin(ang)[None, :, None, :].astype(x.dtype)
            xs = x.reshape(b, s, h, half, 2)
            x0, x1 = (xs[..., 0], xs[..., 1])
            r0 = x0 * cos - x1 * sin
            r1 = x1 * cos + x0 * sin
            return jnp.stack([r0, r1], axis=-1).reshape(b, s, h, d)
        b, s, _ = x.shape
        kv_latent = x @ w_kv_down
        k_c = (kv_latent @ w_kv_up_k).reshape(b, s, HEADS, HEAD_DIM)
        v_c = (kv_latent @ w_kv_up_v).reshape(b, s, HEADS, HEAD_DIM)
        k_r = jnp.broadcast_to((x @ w_k_rope)[:, :, None, :], (b, s, HEADS, HEAD_DIM))
        k_r = apply_rope(k_r)
        k = jnp.concatenate([k_c, k_r], axis=-1)
        q_c = (x @ w_q_down @ w_q_up).reshape(b, s, HEADS, HEAD_DIM)
        q_r = jnp.broadcast_to((x @ w_q_rope)[:, :, None, :], (b, s, HEADS, HEAD_DIM))
        q_r = apply_rope(q_r)
        q = jnp.concatenate([q_c, q_r], axis=-1)
        scale = 1.0 / np.sqrt(2 * HEAD_DIM)
        scores = jnp.einsum('bqhd,bkhd->bhqk', q, k) * scale
        attn = jax.nn.softmax(scores, axis=-1)
        out = jnp.einsum('bhqk,bkhd->bqhd', attn, v_c).reshape(b, s, HEADS * HEAD_DIM)
        return out @ w_out

    def _L0_ffn_ref(x, W1, W2, W3):
        import jax, jax.numpy as jnp
        import numpy as np
        B, S, D, H = (4, 256, 256, 1024)

        def fwht(x):
            orig_shape = x.shape
            n = orig_shape[-1]
            x = x.reshape(-1, n)
            h = 1
            while h < n:
                xb = x.reshape(-1, n // (2 * h), 2, h)
                a = xb[:, :, 0, :]
                b = xb[:, :, 1, :]
                x = jnp.stack([a + b, a - b], axis=2).reshape(-1, n)
                h *= 2
            scale = jnp.asarray(1.0 / np.sqrt(n), dtype=x.dtype)
            return (x * scale).reshape(orig_shape)
        up_gate = jnp.einsum('bsd,hd->bsh', x, W1)
        up_lin = jnp.einsum('bsd,hd->bsh', x, W3)
        hidden = jax.nn.silu(up_gate) * up_lin
        hidden = fwht(hidden)
        out = jnp.einsum('bsh,dh->bsd', hidden, W2)
        return out
    x = L0_attn_x
    mod = (_silu(L0_c) @ L0_wmod).reshape(L0_c.shape[0], 6, 1, -1)
    sa, ca, ga, sb, cb, gb = (mod[:, 0], mod[:, 1], mod[:, 2], mod[:, 3], mod[:, 4], mod[:, 5])
    ga = (2 * (ga >= 0) - 1) * jnp.maximum(jnp.abs(ga), 0.25)
    gb = (2 * (gb >= 0) - 1) * jnp.maximum(jnp.abs(gb), 0.25)
    h = _layernorm(x, axis=-1) * (1 + ca) + sa
    x = x + ga * _L0_attn_ref(h, L0_attn_w_kv_down, L0_attn_w_kv_up_k, L0_attn_w_kv_up_v, L0_attn_w_q_down, L0_attn_w_q_up, L0_attn_w_k_rope, L0_attn_w_q_rope, L0_attn_w_out)
    h = _layernorm(x, axis=-1) * (1 + cb) + sb
    x = x + gb * _L0_ffn_ref(h, L0_ffn_W1, L0_ffn_W2, L0_ffn_W3)
    return x

_drawn_inputs = setup_inputs


def setup_inputs(seed=0):
    import zlib

    import numpy as np

    out = dict(_drawn_inputs(seed))
    spreads = {}
    factors = {'L0_attn_w_k_rope': 4.194, 'L0_attn_w_q_rope': 4.242}
    for name, (base, spread) in spreads.items():
        noise = np.random.default_rng([zlib.crc32(name.encode()), seed]).standard_normal(out[name].shape)
        drawn = base * np.exp(spread * noise) if base else spread * noise
        out[name] = jnp.asarray(drawn.astype(out[name].dtype))
    for name, factor in factors.items():
        out[name] = (out[name] * factor).astype(out[name].dtype)
    return out
```

```python
import concourse.bass as bass
from concourse import mybir
from contextlib import ExitStack


def adaln_block(nc, x_in, ct, wmod, wqd_t, wqu, wkd, wuk, wuv, wrope, wout, w1t, w3t, w2t,
                cos_in, sin_in, ident_in, hada_in, out):
    f32 = mybir.dt.float32
    f32r = mybir.dt.float32r
    ALU = mybir.AluOpType
    ACT = mybir.ActivationFunctionType
    AX = mybir.AxisListType

    P = 128
    B, S, D = x_in.shape
    TT = S // P
    DT = D // P
    HD = cos_in.shape[0] // 2
    HEADS = wqu.shape[1] // HD
    LAT = wkd.shape[1]
    HID = w1t.shape[1]
    HT = HID // P
    J = 4
    NG = HEADS // J
    STEPS = NG * TT
    LEAD = 6
    PART = 2 * HD
    MROW = 3 * PART
    SCALE = float(1.0 / (2 * HD) ** 0.5)
    EPS = 1e-5
    TILES = J * STEPS
    STACK_DMAS = 3 + 6
    LOADED = 16 * STACK_DMAS

    MAXB, SCB, PVB, MA, MB, MC = 0, 2, 4, 5, 6, 7

    ctx = ExitStack()
    sem = lambda name: ctx.enter_context(nc.semaphore(name))
    sb = lambda name, shape, dt=f32: ctx.enter_context(nc.sbuf_tensor(name, shape, dt))

    with ctx:
        ps = ctx.enter_context(nc.psum_tensor("ps", [P, 8, 512], f32))
        x = sb("x", [P, B, TT, D])
        gates = sb("gates", [P, B, 2, D])
        mod_t = sb("mod_t", [P, B, 8])
        ident = sb("ident", [P, P])
        stats = sb("stats", [P, TT, 6])
        mean_var = sb("mean_var", [P, TT, 2])
        var_eps = sb("var_eps", [P, TT])
        rstd = sb("rstd", [P, TT])
        eps_c = sb("eps_c", [P, TT])
        half_c = sb("half_c", [P, TT])
        mod_now = sb("mod_now", [P, 4])
        xn = sb("xn", [P, TT, D])
        y_gated = sb("y_gated", [P, TT, D])

        p1 = ExitStack()
        with p1:
            sb1 = lambda name, shape, dt=f32: p1.enter_context(nc.sbuf_tensor(name, shape, dt))
            s1 = lambda name: p1.enter_context(nc.semaphore(name))
            stack = [sb1(f"stack{g}", [P, J, 2, S], f32r) for g in range(NG)]
            probs = [sb1(f"probs{i}", [P, J, S]) for i in range(2)]
            h_t = sb1("h_t", [P, DT, S])
            parts = sb1("parts", [P, DT, 4, S], f32r)
            Q_LO, Q_HI, K_HI, K_LO = range(4)
            kv_lat = sb1("kv_lat", [LAT, S])
            rope_c, rope_s = sb1("rope_c", [PART, S]), sb1("rope_s", [PART, S])
            r_hi, r_lo = sb1("r_hi", [PART, S], f32r), sb1("r_lo", [PART, S], f32r)
            v_new = sb1("v_new", [P, TT, D])
            v_ones = sb1("v_ones", [P, TT, HEADS, 2 * HD])
            maxima = [sb1(f"maxima{i}", [P, TT, J]) for i in range(2)]
            neg_max = sb1("neg_max", [J, S], f32r)
            pv_sb = sb1("pv_sb", [P, S])
            inv_sum = sb1("inv_sum", [P, TT, J])
            attn = sb1("attn", [P, TT, D])
            attn_t = sb1("attn_t", [P, DT, S])
            cos_sb = sb1("cos_sb", [PART, S])
            sin_sb = sb1("sin_sb", [2 * PART, S])
            wq_sb = sb1("wq_sb", [P, DT, D])
            wkd_sb = sb1("wkd_sb", [P, DT, LAT])
            wuk_sb = sb1("wuk_sb", [LAT, D])
            wuv_sb = sb1("wuv_sb", [LAT, D])
            wrope_sb = sb1("wrope_sb", [P, DT, 2 * PART])
            wout_sb = sb1("wout_sb", [P, DT, D])
            wm = [probs[0], probs[1]]
            QC = wqu.shape[0]
            wqd_sb = attn
            wqu_sb = attn
            ct_sb = pv_sb
            g8 = attn_t
            sel = v_new

            wts = s1("wts")
            x_first, x_second, x_rest = s1("x_first"), s1("x_second"), s1("x_rest")
            consts = s1("consts")
            silu_c = s1("silu_c")
            mod_psum, mod_sb = s1("mod_psum"), s1("mod_sb")
            gate_psum, gate_sb = s1("gate_psum"), s1("gate_sb")
            gate_sign, gate_abs = s1("gate_sign"), s1("gate_abs")
            bc_full, bc_free = s1("bc_full"), s1("bc_free")
            max_full, max_free = s1("max_full"), s1("max_free")
            sc_full, exp_done = s1("sc_full"), s1("exp_done")
            pv_done, pv_copied = s1("pv_done"), s1("pv_copied")
            misc_full = {b: s1(f"misc_full{b}") for b in (MA, MB, MC)}
            stats_done, aggr_done = s1("stats_done"), s1("aggr_done")
            eps_added, rstd_done, xn_done = s1("eps_added"), s1("rstd_done"), s1("xn_done")
            mod_copied = s1("mod_copied")
            h_ready, kv_ready = s1("h_ready"), s1("kv_ready")
            rope_mul, rope_added = s1("rope_mul"), s1("rope_added")
            rhi_done, rlo_done = s1("rhi_done"), s1("rlo_done")
            hi_done, lo_done = s1("hi_done"), s1("lo_done")
            v_evac, v_ready = s1("v_evac"), s1("v_ready")
            stack_loaded = [s1(f"stack_loaded{g}") for g in range(NG)]
            neg_ready, max_loaded = s1("neg_ready"), s1("max_loaded")
            recip_done, norm_done = s1("recip_done"), s1("norm_done")
            attn_t_ready = s1("attn_t_ready")
            y_gated_done, x1_done = s1("y_gated_done"), s1("x1_done")

            TASKS = [
                (1, "pvT3", MC, "prev"),
                (2, "hT0", MA, "nxt"), (2, "hT1", MB, "nxt"), (2, "maxT1", MC, "cur"),
                (3, "aT0", MA, "prev"), (3, "aT1", MB, "prev"),
                (4, "rope", MA, "nxt"), (4, "kvlat", MB, "nxt"),
                (5, "q0", MA, "nxt"), (5, "q1", MB, "nxt"), (5, "pvT0", MC, "cur"),
                (6, "k0", MA, "nxt"), (6, "k1", MB, "nxt"), (6, "maxT2", MC, "cur"),
                (7, "out0", MA, "prev"), (7, "out1", MB, "prev"),
                (8, "v0", MA, "nxt"), (8, "v1", MB, "nxt"),
                (9, "pvT1", MC, "cur"), (10, "maxT3", MC, "cur"),
                (13, "pvT2", MC, "cur"), (14, "maxT0", MC, "nxt"),
            ]

            class Body:

                def __init__(self, b, kinds):
                    self.b, self.kinds = b, kinds
                    self.prev, self.cur, self.nxt = (k in kinds for k in ("prev", "cur", "nxt"))
                    self.tasks = [t for t in TASKS if t[3] in kinds]

                def at(self, step):
                    return [name for s, name, _, _ in self.tasks if s == step]

                def bank(self, name):
                    return next(t[2] for t in TASKS if t[1] == name)

                def used(self, name):
                    bank = self.bank(name)
                    here = [t[1] for t in self.tasks if t[2] == bank].index(name)
                    count = lambda *kinds: sum(t[2] == bank and t[3] in kinds for t in TASKS)
                    n, m, k = count("nxt"), count("nxt", "cur"), count("nxt", "cur", "prev")
                    if self.kinds == ("nxt",):
                        return here
                    if self.kinds == ("cur", "nxt"):
                        return n + here
                    if self.kinds == ("prev",):
                        return n + m + (B - 2) * k + count("prev", "cur") + here
                    return self.b * k + (n + m - k + here)

            def bank_read(name, n):
                i = int(name[-1]) if name[-1].isdigit() else 0
                if name == "rope":
                    return rope_mul, 2 * n + 2
                if name == "kvlat":
                    return kv_ready, n + 1
                kind, each = {"hT": (h_ready, DT), "aT": (attn_t_ready, DT), "q": (lo_done, 4), "k": (lo_done, 4),
                              "v": (v_evac, 2), "out": (y_gated_done, 2), "pvT": (norm_done, NG),
                              "maxT": (neg_ready, NG)}[name[:-1]]
                return kind, each * n + i + (DT if name[0] == "k" else 0) + 1

            def task_before(k, name):
                bank = k.bank(name)
                sequence = {"prev": k.b - 1, "cur": k.b, "nxt": k.b + 1}
                here = [(t[1], sequence[t[3]]) for t in k.tasks if t[2] == bank]
                at = [t[0] for t in here].index(name)
                if at:
                    return here[at - 1]
                if k.kinds == ("nxt",):
                    return None
                kinds = ("prev", "cur") if k.kinds == ("prev",) else ("prev", "cur", "nxt")
                last = [t for t in TASKS if t[2] == bank and t[3] in kinds][-1]
                return last[1], sequence[last[3]] - 1

            def on(engine, body):
                body(Body(-1, ("nxt",)))
                body(Body(0, ("cur", "nxt")))
                with engine.Fori(1, B - 1) as b:
                    body(Body(b, ("prev", "cur", "nxt")))
                body(Body(B - 1, ("prev", "cur")))
                body(Body(B, ("prev",)))

            def wait(engine, semaphore, value):
                if not isinstance(value, int) or value > 0:
                    engine.wait_ge(semaphore, value)

            def max_at(body, s):
                u = s + LEAD
                if u < STEPS:
                    return (body.b, u // TT, u % TT) if body.cur else None
                return (body.b + 1, (u - STEPS) // TT, u % TT) if body.nxt else None

            block = p1.enter_context(nc.Block())

            @block.sync
            def _(sp):
                sp.dma_start(ct_sb[:, 16:32].rearrange("p (t b) -> p t b", t=DT),
                             ct.rearrange("(t p) b -> p t b", p=P)).then_inc(silu_c, 16)
                for t in range(DT):
                    sp.dma_start(wm[t][:, :, :].rearrange("p j s -> p (j s)")[:, 0:6 * D],
                                 wmod[t * P:(t + 1) * P, :]).then_inc(wts, 16)
                sp.dma_start(ident[:, :], ident_in).then_inc(wts, 16)
                sp.dma_start(x[:, 0, :, :], x_in[0].rearrange("(t p) d -> p t d", p=P)).then_inc(x_first, 16)
                sp.dma_start(wqd_sb[0:QC, 0, :], wqd_t).then_inc(wts, 16)
                sp.dma_start(wqu_sb[0:QC, 1, :], wqu).then_inc(wts, 16)
                sp.dma_start(wkd_sb[:, :, :], wkd.rearrange("(t p) n -> p t n", p=P)).then_inc(wts, 16)
                sp.dma_start(wrope_sb[:, :, :], wrope.rearrange("(t p) n -> p t n", p=P)).then_inc(wts, 16)
                sp.dma_start(wuk_sb[:, :], wuk).then_inc(wts, 16)
                sp.dma_start(wuv_sb[:, :], wuv).then_inc(wts, 16)
                sp.dma_start(cos_sb[:, :], cos_in).then_inc(wts, 16)
                sp.dma_start(sin_sb[PART:2 * PART, :], sin_in).then_inc(wts, 16)
                sp.dma_start(wout_sb[:, :, :], wout.rearrange("(t p) n -> p t n", p=P)).then_inc(wts, 16)
                sp.dma_start(x[:, 1, :, :], x_in[1].rearrange("(t p) d -> p t d", p=P)).then_inc(x_second, 16)
                for b in range(2, B):
                    sp.dma_start(x[:, b, :, :], x_in[b].rearrange("(t p) d -> p t d", p=P)).then_inc(x_rest, 16)

                def move(to, source, signals):
                    sp.dma_start(to.bitcast(f32), source.bitcast(f32)).then_inc(signals, 16)

                def load_stack(n, g, before):
                    if before:
                        wait(sp, sc_full, TILES * (n - 1) + J * TT * (g + 1))
                    wait(sp, lo_done, 4 * (n + 1))
                    wait(sp, rlo_done, n + 1)
                    rows, t = slice(J * HD * (g % 2), J * HD * (g % 2 + 1)), g // 2
                    for part, (first, second) in enumerate(((Q_HI, K_HI), (Q_HI, K_LO), (Q_LO, K_HI))):
                        to = PART * part
                        move(stack[g][to:to + HD, :, :, :].rearrange("p j a s -> p (j a s)"),
                             parts[rows, t, first:second + 1:second - first, :], stack_loaded[g])
                    for part, sources in enumerate(((r_hi, r_hi), (r_hi, r_lo), (r_lo, r_hi))):
                        to = PART * part + HD
                        for a, src in enumerate(sources):
                            move(stack[g][to:to + HD, :, a, :],
                                 src[a * HD:(a + 1) * HD, :].rearrange("p (o s) -> p o s", o=1).to_broadcast([HD, J, S]),
                                 stack_loaded[g])

                def load_max(n, g):
                    wait(sp, neg_ready, NG * n + g + 1)
                    move(stack[g][MROW:MROW + 1, :, 0, :], neg_max[:, :], max_loaded)

                def body(k):
                    if k.cur:
                        load_stack(k.b, NG - 1, k.prev)
                        load_max(k.b, 1)
                        load_max(k.b, 2)
                    if k.nxt:
                        load_stack(k.b + 1, 0, k.cur)
                        load_stack(k.b + 1, 1, k.cur)
                    if k.cur:
                        load_max(k.b, 3)
                    if k.nxt:
                        load_stack(k.b + 1, 2, k.cur)
                        load_max(k.b + 1, 0)

                on(sp, body)

            @block.tensor
            def _(pe):
                pe.wait_ge(wts, 16 * 12)
                pe.wait_ge(silu_c, 17)
                for i, chunk in enumerate((0, 1, 3, 4)):
                    for t in range(DT):
                        col = chunk * D + t * P
                        for kt in range(DT):
                            last = nc.tensor.matmul(ps[:, MA, (i * DT + t) * B:(i * DT + t + 1) * B],
                                                    wm[kt][:, :, :].rearrange("p j s -> p (j s)")[:, col:col + P],
                                                    ct_sb[:, kt * B:(kt + 1) * B],
                                                    start=kt == 0, stop=kt == DT - 1)
                last.then_inc(mod_psum, 1)
                for i, chunk in enumerate((2, 5)):
                    for kt in range(DT):
                        last = nc.tensor.matmul(ps[0:B, MB, i * D:(i + 1) * D], ct_sb[:, kt * B:(kt + 1) * B],
                                                wm[kt][:, :, :].rearrange("p j s -> p (j s)")[:, chunk * D:(chunk + 1) * D],
                                                start=kt == 0, stop=kt == DT - 1)
                last.then_inc(gate_psum, 1)
                for t in range(DT):
                    last = nc.tensor.matmul(ps[:, MC, t * D:(t + 1) * D], wqd_sb[0:QC, 0, t * P:(t + 1) * P],
                                            wqu_sb[0:QC, 1, :], start=True, stop=True)
                last.then_inc(mod_psum, 1)
                pe.wait_ge(gate_sb, 2)
                for b in range(B):
                    if b >= 2:
                        pe.wait_ge(bc_free, b - 1)
                    one_row = sel[0:B, :, :].rearrange("p t d -> p (t d)")[:, b * P:(b + 1) * P]
                    nc.tensor.matmul(ps[:, SCB + b % 2, :], one_row, g8[0:B, 0, :], start=True, stop=True).then_inc(bc_full, 1)

                def task(k, name):
                    bank = k.bank(name)
                    before = task_before(k, name)
                    if before:
                        wait(pe, *bank_read(*before))
                    n = int(name[-1]) if name[-1].isdigit() else 0
                    if name[:2] == "hT":
                        wait(pe, xn_done, TT * (k.b + 2))
                        for t in range(TT):
                            last = nc.tensor.transpose(ps[:, bank, t * P:(t + 1) * P], xn[:, t, n * P:(n + 1) * P], ident[:, :])
                    elif name == "rope":
                        wait(pe, h_ready, DT * (k.b + 2))
                        for t in range(DT):
                            last = nc.tensor.matmul(ps[0:2 * PART, bank, :], wrope_sb[:, t, :], h_t[:, t, :],
                                                    start=t == 0, stop=t == DT - 1)
                    elif name == "kvlat":
                        for t in range(DT):
                            last = nc.tensor.matmul(ps[0:LAT, bank, :], wkd_sb[:, t, :], h_t[:, t, :],
                                                    start=t == 0, stop=t == DT - 1)
                    elif name[0] == "q":
                        for t in range(DT):
                            last = nc.tensor.matmul(ps[:, bank, :], wq_sb[:, t, n * P:(n + 1) * P], h_t[:, t, :],
                                                    start=t == 0, stop=t == DT - 1)
                    elif name[0] == "k":
                        wait(pe, kv_ready, k.b + 2)
                        last = nc.tensor.matmul(ps[:, bank, :], wuk_sb[:, n * P:(n + 1) * P], kv_lat[:, :],
                                                start=True, stop=True)
                    elif name[0] == "v":
                        for i in range(2):
                            t = 2 * n + i
                            last = nc.tensor.matmul(ps[:, bank, i * D:(i + 1) * D], kv_lat[:, t * P:(t + 1) * P],
                                                    wuv_sb[:, :], start=True, stop=True)
                    elif name[:4] == "maxT":
                        nb = k.b + 1 if n == 0 else k.b
                        wait(pe, max_free, TILES * nb + J * TT * (n + 1))
                        for t in range(TT):
                            last = nc.tensor.transpose(ps[0:J, bank, t * P:(t + 1) * P], maxima[n % 2][:, t, :], ident[:, :])
                    elif name[:3] == "pvT":
                        nb = k.b - 1 if n == NG - 1 else k.b
                        wait(pe, pv_copied, NG * nb + n + 1)
                        for t in range(TT):
                            last = nc.tensor.transpose(ps[:, bank, t * P:(t + 1) * P], pv_sb[:, t * P:(t + 1) * P], ident[:, :])
                    elif name[:2] == "aT":
                        wait(pe, norm_done, NG * k.b)
                        for t in range(TT):
                            last = nc.tensor.transpose(ps[:, bank, t * P:(t + 1) * P], attn[:, t, n * P:(n + 1) * P], ident[:, :])
                    else:
                        wait(pe, attn_t_ready, DT * k.b)
                        for i in range(2):
                            t = 2 * n + i
                            for kt in range(DT):
                                last = nc.tensor.matmul(ps[:, bank, i * D:(i + 1) * D], attn_t[:, kt, t * P:(t + 1) * P],
                                                        wout_sb[:, kt, :], start=kt == 0, stop=kt == DT - 1)
                    last.then_inc(misc_full[bank], 1)

                def body(k):
                    for s in range(STEPS):
                        g, kt = divmod(s, TT)
                        ahead = max_at(k, s)

                        def max_tile(j):
                            n, mg, qt = ahead
                            if qt == 0 and j == 0:
                                wait(pe, stack_loaded[mg], LOADED * (n + 1))
                            tile = TILES * n + J * (TT * mg + qt) + j
                            wait(pe, max_free, tile - 1)
                            nc.tensor.matmul(ps[:, MAXB + j % 2, :], stack[mg][0:MROW, j, 0, qt * P:(qt + 1) * P],
                                             stack[mg][0:MROW, j, 1, :], start=True, stop=True).then_inc(max_full, 1)

                        def score_tile(j):
                            if kt == 0 and j == 0:
                                wait(pe, max_loaded, 16 * (NG * k.b + g + 1))
                            tile = TILES * k.b + J * s + j
                            wait(pe, exp_done, tile - 1)
                            nc.tensor.matmul(ps[:, SCB + j % 2, :], stack[g][0:MROW + 1, j, 1, kt * P:(kt + 1) * P],
                                             stack[g][0:MROW + 1, j, 0, :], start=True, stop=True).then_inc(sc_full, 1)

                        def prob_v():
                            pg, pt = divmod((s - 1) % STEPS, TT)
                            ended = STEPS * k.b + s
                            wait(pe, exp_done, J * ended)
                            if pt == 0:
                                group = (NG * k.b + pg) if s else None
                                wait(pe, v_ready, group + 1)
                                wait(pe, pv_copied, group)
                            for j in range(J):
                                last = nc.tensor.matmul(ps[2 * HD * j:2 * HD * (j + 1), PVB, :],
                                                        v_ones[:, pt, J * pg + j, :], probs[(s - 1) % 2][:, j, :],
                                                        start=pt == 0, stop=pt == TT - 1)
                            last.then_inc(pv_done, 1)

                        for half in (0, 2):
                            for j in (half, half + 1):
                                if ahead:
                                    max_tile(j)
                                if k.cur:
                                    score_tile(j)
                            if half == 0 and (k.prev if s == 0 else k.cur):
                                prob_v()
                        for name in k.at(s):
                            task(k, name)

                pe.wait_ge(consts, NG + 2)
                pe.wait_ge(mod_sb, 5)
                pe.wait_ge(bc_free, B)
                on(pe, body)

            @block.scalar
            def _(act):
                act.wait_ge(silu_c, 16)
                nc.scalar.activation(ct_sb[:, 0:16], ct_sb[:, 16:32], ACT.Silu).then_inc(silu_c, 1)
                act.wait_ge(mod_psum, 2)
                nc.scalar.copy(wq_sb[:, :, :].rearrange("p t d -> p (t d)"), ps[:, MC, :]).then_inc(mod_sb, 1)
                for b in range(B):
                    act.wait_ge(bc_full, b + 1)
                    nc.scalar.copy(gates[:, b, :, :].rearrange("p a d -> p (a d)"), ps[:, SCB + b % 2, :]).then_inc(bc_free, 1)

                def body(k):
                    for s in range(STEPS):
                        g, kt = divmod(s, TT)
                        if k.cur:
                            for j in range(J):
                                tile = TILES * k.b + J * s + j
                                act.wait_ge(sc_full, tile + 1)
                                if j == 0:
                                    wait(act, pv_done, STEPS * k.b + s - 1)
                                nc.scalar.activation(probs[s % 2][:, j, :], ps[:, SCB + j % 2, :], ACT.Exp,
                                                     scale=SCALE).then_inc(exp_done, 1)
                        if kt == 0 and (k.prev if s == 0 else k.cur):
                            group = NG * k.b + g
                            act.wait_ge(pv_done, TT * group)
                            wait(act, norm_done, group - 1)
                            nc.scalar.copy(pv_sb[:, :], ps[:, PVB, :]).then_inc(pv_copied, 1)
                        for name in k.at(s):
                            bank = k.bank(name)
                            n = int(name[-1]) if name[-1].isdigit() else 0
                            if name[:2] == "hT":
                                if n == 0:
                                    act.wait_ge(mod_copied, k.b + 2)
                                act.wait_ge(misc_full[bank], k.used(name) + 1)
                                nc.scalar.activation(h_t[:, n, :], ps[:, bank, :], ACT.Identity,
                                                     scale=mod_now[:, 2 + n:3 + n], bias=mod_now[:, n:n + 1]).then_inc(h_ready, 1)
                            elif name[:2] == "aT":
                                act.wait_ge(misc_full[bank], k.used(name) + 1)
                                nc.scalar.copy(attn_t[:, n, :], ps[:, bank, :]).then_inc(attn_t_ready, 1)
                            elif name == "kvlat":
                                act.wait_ge(misc_full[bank], k.used(name) + 1)
                                nc.scalar.copy(kv_lat[:, :], ps[0:LAT, bank, :]).then_inc(kv_ready, 1)
                            elif name[0] in "qk":
                                wait(act, stack_loaded[2 * n + 1], LOADED * (k.b + 1))
                                act.wait_ge(misc_full[bank], k.used(name) + 1)
                                nc.scalar.copy(parts[:, n, Q_HI if name[0] == "q" else K_HI, :], ps[:, bank, :]).then_inc(hi_done, 1)
                            elif name[0] == "v":
                                wait(act, v_ready, NG * (k.b + 1))
                                act.wait_ge(misc_full[bank], k.used(name) + 1)
                                nc.scalar.copy(v_new[:, 2 * n:2 * n + 2, :], ps[:, bank, :].rearrange("p (t d) -> p t d", t=2)).then_inc(v_evac, 1)

                on(act, body)

            @block.vector
            def _(dve):
                for g in range(NG):
                    nc.vector.memset(stack[g][MROW:MROW + 1, :, 1, :].bitcast(f32), 1.0).then_inc(consts, 1)
                nc.vector.memset(eps_c[:, :], EPS)
                nc.vector.memset(half_c[:, :], -0.5).then_inc(consts, 1)
                dve.wait_ge(mod_psum, 1)
                modp = ps[:, MA, 0:8 * B].rearrange("p (i b) -> p b i", b=B)
                for i in range(4):
                    nc.vector.tensor_scalar(mod_t[:, :, 2 * i:2 * i + 2], modp[:, :, 2 * i:2 * i + 2],
                                            float(i % 2), None, ALU.add).then_inc(mod_sb, 1)
                dve.wait_ge(gate_psum, 1)
                sign, gate = g8[0:B, 1, :], g8[0:B, 0, :]
                nc.vector.tensor_scalar(sign, ps[0:B, MB, :], 0.0, 2.0, ALU.is_ge, ALU.mult).then_inc(gate_sign, 1)
                dve.wait_ge(gate_sign, 1)
                nc.vector.tensor_scalar(sign, sign, -1.0, None, ALU.add).then_inc(gate_sign, 1)
                dve.wait_ge(gate_sign, 2)
                nc.vector.tensor_tensor(gate, ps[0:B, MB, :], sign, ALU.mult).then_inc(gate_abs, 1)
                dve.wait_ge(gate_abs, 1)
                nc.vector.scalar_tensor_tensor(out=gate, in0=gate, scalar=0.25, in1=sign,
                                               op0=ALU.max, op1=ALU.mult).then_inc(gate_sb, 1)

                def body(k):
                    for s in range(STEPS):
                        ahead = max_at(k, s)
                        if ahead:
                            n, mg, qt = ahead
                            for j in range(J):
                                dve.wait_ge(max_full, TILES * n + J * (TT * mg + qt) + j + 1)
                                nc.vector.tensor_reduce(out=maxima[mg % 2][:, qt, j:j + 1], in_=ps[:, MAXB + j % 2, :],
                                                        axis=AX.X, op=ALU.max).then_inc(max_free, 1)
                        if s == 0 and k.nxt:
                            if not k.cur:
                                dve.wait_ge(x_first, 16)
                                dve.wait_ge(mod_sb, 5)
                            elif not k.prev:
                                dve.wait_ge(x_second, 16)
                                dve.wait_ge(x_rest, 16 * (B - 2))
                            wait(dve, h_ready, DT * (k.b + 1))
                            for t in range(TT):
                                nc.vector.bn_stats(stats[:, t, :], x[:, k.b + 1, t, :]).then_inc(stats_done, 1)
                            dve.wait_ge(stats_done, TT * (k.b + 2))
                            nc.vector.tensor_copy(mod_now[:, :], mod_t[:, k.b + 1, 0:4]).then_inc(mod_copied, 1)
                            for t in range(TT):
                                nc.vector.bn_aggr(mean_var[:, t, :], stats[:, t, :]).then_inc(aggr_done, 1)
                        if s == 1 and k.nxt:
                            dve.wait_ge(rstd_done, k.b + 2)
                            for t in range(TT):
                                nc.vector.tensor_scalar(xn[:, t, :], x[:, k.b + 1, t, :], mean_var[:, t, 0:1],
                                                        rstd[:, t:t + 1], ALU.subtract, ALU.mult).then_inc(xn_done, 1)
                        for name in k.at(s):
                            bank = k.bank(name)
                            n = int(name[-1]) if name[-1].isdigit() else 0
                            if name[:3] == "pvT":
                                nb = k.b - 1 if n == NG - 1 else k.b
                                group = NG * nb + n
                                dve.wait_ge(misc_full[bank], k.used(name) + 1)
                                pv = ps[:, bank, :].rearrange("p (t j d) -> p t j d", t=TT, j=J)
                                nc.vector.reciprocal(inv_sum[:, :, :], pv[:, :, :, HD]).then_inc(recip_done, 1)
                                if n == 0:
                                    wait(dve, attn_t_ready, DT * nb)
                                dve.wait_ge(recip_done, group + 1)
                                to = attn[:, :, J * HD * n:J * HD * (n + 1)].rearrange("p t (j d) -> p t j d", j=J)
                                inv = inv_sum[:, :, :].rearrange("p t (j o) -> p t j o", o=1).to_broadcast([P, TT, J, HD])
                                nc.vector.tensor_tensor(to, pv[:, :, :, 0:HD], inv, ALU.mult).then_inc(norm_done, 1)
                            elif name[:4] == "maxT":
                                nb = k.b + 1 if n == 0 else k.b
                                wait(dve, max_loaded, 16 * (NG * nb + n))
                                dve.wait_ge(misc_full[bank], k.used(name) + 1)
                                nc.vector.tensor_scalar(neg_max[:, :], ps[0:J, bank, :], -1.0, None, ALU.mult).then_inc(neg_ready, 1)
                            elif name == "rope":
                                wait(dve, rlo_done, k.b + 1)
                                dve.wait_ge(misc_full[bank], k.used(name) + 1)
                                nc.vector.tensor_tensor(rope_c[:, :], ps[0:PART, bank, :], cos_sb[:, :], ALU.mult).then_inc(rope_mul, 1)
                                nc.vector.tensor_tensor(rope_s[:, :], ps[PART:2 * PART, bank, :], sin_sb[PART:2 * PART, :], ALU.mult).then_inc(rope_mul, 1)
                            elif name[:3] == "out":
                                wait(dve, x1_done, 2 * (k.b - 1))
                                dve.wait_ge(misc_full[bank], k.used(name) + 1)
                                ga = gates[:, k.b - 1, 0:1, :].to_broadcast([P, 2, D])
                                nc.vector.tensor_tensor(y_gated[:, 2 * n:2 * n + 2, :], ps[:, bank, :].rearrange("p (t d) -> p t d", t=2),
                                                        ga, ALU.mult).then_inc(y_gated_done, 1)
                            elif name[0] in "qk" and name != "kvlat":
                                order = (0 if name[0] == "q" else 2) + n
                                hi, lo = (parts[:, n, i, :] for i in ((Q_HI, Q_LO) if name[0] == "q" else (K_HI, K_LO)))
                                wait(dve, stack_loaded[2 * n + 1], LOADED * (k.b + 1))
                                dve.wait_ge(hi_done, 4 * (k.b + 1) + order + 1)
                                nc.vector.tensor_tensor(lo, ps[:, bank, :], hi.bitcast(f32), ALU.subtract).then_inc(lo_done, 1)

                on(dve, body)

            @block.gpsimd
            def _(pool):
                nc.gpsimd.memset(v_ones[:, :, :, HD:2 * HD], 1.0).then_inc(consts, 1)
                pool.wait_ge(wts, 16 * 12)
                pool.wait_ge(consts, NG + 2)
                nc.gpsimd.tensor_copy(sel[0:B, :, :].rearrange("p t (a d) -> p (t a) d", d=P),
                                      ident[0:B, 0:B].rearrange("p (b o) -> p b o", o=1).to_broadcast([B, B, P])).then_inc(gate_sb, 1)

                def copy_v(n, g, waits):
                    wait(pool, v_evac, 2 * (n + 1))
                    if waits:
                        wait(pool, pv_done, STEPS * (n - 1) + TT * (g + 1))
                    new = v_new[:, :, J * HD * g:J * HD * (g + 1)].rearrange("p t (j d) -> p t j d", j=J)
                    place = v_ones[:, :, J * g:J * (g + 1), :]
                    nc.gpsimd.tensor_tensor(place[:, :, :, 0:HD], new, place[:, :, :, HD:2 * HD], ALU.mult).then_inc(v_ready, 1)

                def body(k):
                    if k.nxt:
                        pool.wait_ge(aggr_done, TT * (k.b + 2))
                        wait(pool, xn_done, TT * (k.b + 1))
                        nc.gpsimd.tensor_tensor(var_eps[:, :], mean_var[:, :, 1], eps_c[:, :], ALU.add).then_inc(eps_added, 1)
                        pool.wait_ge(eps_added, k.b + 2)
                        nc.gpsimd.tensor_tensor(rstd[:, :], var_eps[:, :], half_c[:, :], ALU.pow).then_inc(rstd_done, 1)
                    if k.cur:
                        copy_v(k.b, NG - 1, k.prev)
                    if k.nxt:
                        wait(pool, stack_loaded[NG - 1], LOADED * (k.b + 1))
                        pool.wait_ge(rope_mul, 2 * (k.b + 2))
                        nc.gpsimd.tensor_tensor(r_hi[:, :], rope_c[:, :], rope_s[:, :], ALU.add).then_inc(rhi_done, 1)
                        pool.wait_ge(rhi_done, k.b + 2)
                        nc.gpsimd.tensor_tensor(rope_c[:, :], rope_c[:, :], rope_s[:, :], ALU.add).then_inc(rope_added, 1)
                        pool.wait_ge(rope_added, k.b + 2)
                        nc.gpsimd.tensor_tensor(r_lo[:, :], rope_c[:, :], r_hi[:, :].bitcast(f32), ALU.subtract).then_inc(rlo_done, 1)
                    if k.prev:
                        for n in range(2):
                            pool.wait_ge(y_gated_done, 2 * (k.b - 1) + n + 1)
                            here = x[:, k.b - 1, 2 * n:2 * n + 2, :]
                            nc.gpsimd.tensor_tensor(here, here, y_gated[:, 2 * n:2 * n + 2, :], ALU.add).then_inc(x1_done, 1)
                    if k.nxt:
                        for g in range(NG - 1):
                            copy_v(k.b + 1, g, k.cur)

                on(pool, body)

        p2 = ExitStack()
        with p2:
            sb2 = lambda name, shape, dt=f32: p2.enter_context(nc.sbuf_tensor(name, shape, dt))
            s2 = lambda name: p2.enter_context(nc.semaphore(name))
            w1_hi, w1_lo = sb2("w1_hi", [P, DT, HID], f32r), sb2("w1_lo", [P, DT, HID], f32r)
            w3_hi, w3_lo = sb2("w3_hi", [P, DT, HID], f32r), sb2("w3_lo", [P, DT, HID], f32r)
            w2_hi, w2_lo = sb2("w2_hi", [P, HT, D], f32r), sb2("w2_lo", [P, HT, D], f32r)
            w1_raw, w3_raw = sb2("w1_raw", [P, DT, HID]), sb2("w3_raw", [P, DT, HID])
            w2_raw, w2_mix = sb2("w2_raw", [P, HT, D]), sb2("w2_mix", [P, HT, D])
            hada = sb2("hada", [P, P])
            h2 = sb2("h2", [P, DT, S])
            h2_hi, h2_lo = sb2("h2_hi", [P, DT, S], f32r), sb2("h2_lo", [P, DT, S], f32r)
            silu_sb = [sb2(f"silu_sb{i}", [P, S]) for i in range(2)]
            hid = [sb2(f"hid{i}", [P, S]) for i in range(2)]
            hid_hi, hid_lo = sb2("hid_hi", [P, HT, S], f32r), sb2("hid_lo", [P, HT, S], f32r)

            w_loaded = [s2(f"w_loaded{i}") for i in range(3)]
            w13_hi, w13_lo = s2("w13_hi"), s2("w13_lo")
            fw_full, fw_scaled, fw_stage = s2("fw_full"), s2("fw_scaled"), s2("fw_stage")
            w2_hi_done, w2_lo_done = s2("w2_hi_done"), s2("w2_lo_done")
            stats2, aggr2, eps2, rstd2, xn2 = (s2(n) for n in ("stats2", "aggr2", "eps2", "rstd2", "xn2"))
            mod2 = s2("mod2")
            t_full, h2_ready, h2_hi_done, h2_lo_done = (s2(n) for n in ("t_full", "h2_ready", "h2_hi_done", "h2_lo_done"))
            gate_full, up_full, silu_done, hid_done = (s2(n) for n in ("gate_full", "up_full", "silu_done", "hid_done"))
            hid_hi_done, hid_lo_done = s2("hid_hi_done"), s2("hid_lo_done")
            out_full, out_free, res_done, stored = (s2(n) for n in ("out_full", "out_free", "res_done", "stored"))
            GB, UB, OB = 0, 2, 4
            TRANSPOSE_AT = 4

            def on2(engine, body):
                body(0, True)
                with engine.Fori(1, B - 1) as b:
                    body(b, True)
                body(B - 1, False)

            def wait2(engine, semaphore, value):
                if not isinstance(value, int) or value > 0:
                    engine.wait_ge(semaphore, value)

            block2 = p2.enter_context(nc.Block())

            @block2.sync
            def _(sp):
                sp.dma_start(w1_raw[:, :, :], w1t.rearrange("(t p) h -> p t h", p=P)).then_inc(w_loaded[0], 16)
                sp.dma_start(w3_raw[:, :, :], w3t.rearrange("(t p) h -> p t h", p=P)).then_inc(w_loaded[1], 16)
                sp.dma_start(w2_raw[:, :, :], w2t.rearrange("(t p) d -> p t d", p=P)).then_inc(w_loaded[2], 16)
                sp.dma_start(hada[:, :], hada_in).then_inc(w_loaded[2], 16)
                for b in range(B):
                    sp.wait_ge(res_done, TT * (b + 1))
                    sp.dma_start(out[b].rearrange("(t p) d -> p t d", p=P), x[:, b, :, :]).then_inc(stored, 16)
                sp.wait_ge(stored, 16 * B)

            @block2.tensor
            def _(pe):
                def transposes(n):
                    pe.wait_ge(xn2, TT * (n + 1))
                    for t2 in range(DT):
                        for t in range(TT):
                            last = nc.tensor.transpose(ps[:, OB + t2, t * P:(t + 1) * P], xn[:, t, t2 * P:(t2 + 1) * P], ident[:, :])
                        last.then_inc(t_full, 1)

                transposes(0)
                pe.wait_ge(w_loaded[2], 32)
                w2_flat = w2_raw[:, :, :].rearrange("p t d -> p (t d)")
                for i in range(HT * D // 512):
                    bank = OB + (2 + i) % 4
                    if i >= 2:
                        pe.wait_ge(h2_ready, i - 1)
                    nc.tensor.matmul(ps[:, bank, :], hada[:, :], w2_flat[:, i * 512:(i + 1) * 512],
                                     start=True, stop=True).then_inc(fw_full, 1)
                pe.wait_ge(w13_hi, 2)
                pe.wait_ge(w13_lo, 2)
                pe.wait_ge(fw_scaled, HT * D // 512)

                def split_product(dst, w_parts, x_parts, w_at, x_at, kts):
                    terms = [(w_parts[i], x_parts[j], kt) for i, j in ((0, 0), (1, 0), (0, 1)) for kt in range(kts)]
                    for i, (w, v, kt) in enumerate(terms):
                        last = nc.tensor.matmul(dst, w[:, kt, w_at], v[:, kt, x_at], start=i == 0, stop=i == len(terms) - 1)
                    return last

                def body(b, nxt):
                    pe.wait_ge(h2_hi_done, b + 1)
                    pe.wait_ge(h2_lo_done, b + 1)
                    for m in range(HT):
                        cols = slice(m * P, (m + 1) * P)
                        wait2(pe, silu_done, HT * b + m - 1)
                        split_product(ps[:, GB + m % 2, :], (w1_hi, w1_lo), (h2_hi, h2_lo), cols, slice(0, S), DT).then_inc(gate_full, 1)
                        wait2(pe, hid_done, HT * b + m - 1)
                        split_product(ps[:, UB + m % 2, :], (w3_hi, w3_lo), (h2_hi, h2_lo), cols, slice(0, S), DT).then_inc(up_full, 1)
                        if m == TRANSPOSE_AT and nxt:
                            pe.wait_ge(out_free, TT * b)
                            transposes(b + 1)
                    pe.wait_ge(h2_ready, DT * (b + 2) if nxt else DT * (b + 1))
                    wait2(pe, out_free, TT * b)
                    for m in range(HT):
                        if m == 0:
                            pe.wait_ge(w2_hi_done, 1)
                            pe.wait_ge(w2_lo_done, 1)
                        pe.wait_ge(hid_hi_done, HT * b + m + 1)
                        pe.wait_ge(hid_lo_done, HT * b + m + 1)
                        for t in range(TT):
                            rows = slice(t * P, (t + 1) * P)
                            terms = ((hid_hi, w2_hi), (hid_lo, w2_hi), (hid_hi, w2_lo))
                            for i, (h, w) in enumerate(terms):
                                last = nc.tensor.matmul(ps[:, OB + t, 0:D], h[:, m, rows], w[:, m, :],
                                                        start=m == 0 and i == 0, stop=m == HT - 1 and i == 2)
                            if m == HT - 1:
                                last.then_inc(out_full, 1)

                on2(pe, body)

            @block2.scalar
            def _(act):
                def modulate(n):
                    act.wait_ge(mod2, n + 1)
                    wait2(act, h2_lo_done, n)
                    for t2 in range(DT):
                        act.wait_ge(t_full, DT * n + t2 + 1)
                        nc.scalar.activation(h2[:, t2, :], ps[:, OB + t2, :], ACT.Identity,
                                             scale=mod_now[:, 2 + t2:3 + t2], bias=mod_now[:, t2:t2 + 1]).then_inc(h2_ready, 1)

                def split_h2(n):
                    wait2(act, up_full, HT * n)
                    act.wait_ge(h2_ready, DT * (n + 1))
                    nc.scalar.copy(h2_hi[:, :, :], h2[:, :, :]).then_inc(h2_hi_done, 1)

                modulate(0)
                split_h2(0)
                act.wait_ge(w_loaded[0], 16)
                nc.scalar.copy(w1_hi[:, :, :], w1_raw[:, :, :]).then_inc(w13_hi, 1)
                act.wait_ge(w_loaded[1], 16)
                nc.scalar.copy(w3_hi[:, :, :], w3_raw[:, :, :]).then_inc(w13_hi, 1)
                for i in range(HT * D // 512):
                    bank = OB + (2 + i) % 4
                    act.wait_ge(fw_full, i + 1)
                    nc.scalar.activation(w2_mix[:, :, :].rearrange("p t d -> p (t d)")[:, i * 512:(i + 1) * 512],
                                         ps[:, bank, :], ACT.Copy, scale=float(HID ** -0.5)).then_inc(fw_scaled, 1)
                act.wait_ge(fw_stage, 6)
                nc.scalar.copy(w2_hi[:, :, :], w2_raw[:, :, :]).then_inc(w2_hi_done, 1)

                def body(b, nxt):
                    for m in range(HT + 1):
                        if m < HT:
                            act.wait_ge(gate_full, HT * b + m + 1)
                            wait2(act, hid_done, HT * b + m - 1)
                            nc.scalar.activation(silu_sb[m % 2][:, :], ps[:, GB + m % 2, :], ACT.Silu).then_inc(silu_done, 1)
                        if m >= 1:
                            act.wait_ge(hid_done, HT * b + m)
                            nc.scalar.copy(hid_hi[:, m - 1, :], hid[(m - 1) % 2][:, :]).then_inc(hid_hi_done, 1)
                        if m == TRANSPOSE_AT + 1 and nxt:
                            modulate(b + 1)
                    if nxt:
                        split_h2(b + 1)
                on2(act, body)

            @block2.vector
            def _(dve):
                def layer_norm(n):
                    wait2(dve, h2_ready, DT * n)
                    for t in range(TT):
                        nc.vector.bn_stats(stats[:, t, :], x[:, n, t, :]).then_inc(stats2, 1)
                    dve.wait_ge(stats2, TT * (n + 1))
                    nc.vector.tensor_copy(mod_now[:, :], mod_t[:, n, 4:8]).then_inc(mod2, 1)
                    for t in range(TT):
                        nc.vector.bn_aggr(mean_var[:, t, :], stats[:, t, :]).then_inc(aggr2, 1)

                def normalise(n):
                    dve.wait_ge(rstd2, n + 1)
                    for t in range(TT):
                        nc.vector.tensor_scalar(xn[:, t, :], x[:, n, t, :], mean_var[:, t, 0:1],
                                                rstd[:, t:t + 1], ALU.subtract, ALU.mult).then_inc(xn2, 1)

                def split_h2(n):
                    dve.wait_ge(h2_hi_done, n + 1)
                    wait2(dve, up_full, HT * n)
                    nc.vector.tensor_tensor(h2_lo[:, :, :], h2[:, :, :], h2_hi[:, :, :].bitcast(f32), ALU.subtract).then_inc(h2_lo_done, 1)

                layer_norm(0)
                normalise(0)
                split_h2(0)
                for i, (lo, raw, hi) in enumerate(((w1_lo, w1_raw, w1_hi), (w3_lo, w3_raw, w3_hi))):
                    dve.wait_ge(w13_hi, i + 1)
                    nc.vector.tensor_tensor(lo[:, :, :], raw[:, :, :], hi[:, :, :].bitcast(f32), ALU.subtract).then_inc(w13_lo, 1)
                dve.wait_ge(fw_scaled, HT * D // 512)
                src, dst = w2_mix, w2_raw
                for stage in range(3):
                    h = 1 << stage
                    a, c = (v[:, :, :].rearrange("p (n two h) d -> p n two (h d)", two=2, h=h) for v in (src, dst))
                    if stage:
                        dve.wait_ge(fw_stage, 2 * stage)
                    nc.vector.tensor_tensor(c[:, :, 0, :], a[:, :, 0, :], a[:, :, 1, :], ALU.add).then_inc(fw_stage, 1)
                    nc.vector.tensor_tensor(c[:, :, 1, :], a[:, :, 0, :], a[:, :, 1, :], ALU.subtract).then_inc(fw_stage, 1)
                    src, dst = dst, src
                dve.wait_ge(w2_hi_done, 1)
                nc.vector.tensor_tensor(w2_lo[:, :, :], w2_raw[:, :, :], w2_hi[:, :, :].bitcast(f32), ALU.subtract).then_inc(w2_lo_done, 1)

                def body(b, nxt):
                    for m in range(HT + 1):
                        if m < HT:
                            dve.wait_ge(silu_done, HT * b + m + 1)
                            dve.wait_ge(up_full, HT * b + m + 1)
                            wait2(dve, hid_lo_done, HT * b + m - 1)
                            nc.vector.tensor_tensor(hid[m % 2][:, :], ps[:, UB + m % 2, :], silu_sb[m % 2][:, :], ALU.mult).then_inc(hid_done, 1)
                        if m >= 1:
                            dve.wait_ge(hid_hi_done, HT * b + m)
                            nc.vector.tensor_tensor(hid_lo[:, m - 1, :], hid[(m - 1) % 2][:, :],
                                                    hid_hi[:, m - 1, :].bitcast(f32), ALU.subtract).then_inc(hid_lo_done, 1)
                        if nxt and m == 1:
                            layer_norm(b + 1)
                        if nxt and m == 2:
                            normalise(b + 1)
                    if nxt:
                        split_h2(b + 1)
                    for t in range(TT):
                        dve.wait_ge(out_full, TT * b + t + 1)
                        wait2(dve, res_done, TT * b)
                        nc.vector.tensor_tensor(y_gated[:, t, :], ps[:, OB + t, 0:D], gates[:, b, 1, :], ALU.mult).then_inc(out_free, 1)
                on2(dve, body)

            @block2.gpsimd
            def _(pool):
                def inverse_deviation(n):
                    pool.wait_ge(aggr2, TT * (n + 1))
                    wait2(pool, xn2, TT * n)
                    nc.gpsimd.tensor_tensor(var_eps[:, :], mean_var[:, :, 1], eps_c[:, :], ALU.add).then_inc(eps2, 1)
                    pool.wait_ge(eps2, n + 1)
                    nc.gpsimd.tensor_tensor(rstd[:, :], var_eps[:, :], half_c[:, :], ALU.pow).then_inc(rstd2, 1)
                inverse_deviation(0)
                def body(b, nxt):
                    if nxt:
                        inverse_deviation(b + 1)
                    for t in range(TT):
                        pool.wait_ge(out_free, TT * b + t + 1)
                        here = x[:, b, t, :]
                        nc.gpsimd.tensor_tensor(here, here, y_gated[:, t, :], ALU.add).then_inc(res_done, 1)
                on2(pool, body)


def kernel(**inputs):
    import numpy as np
    import concourse.bacc as bacc
    from concourse.bass_utils import run_bass_kernel_spmd

    arr = {n: np.ascontiguousarray(v) for n, v in inputs.items()}
    S, HD = arr["L0_attn_x"].shape[1], arr["L0_attn_w_k_rope"].shape[1]
    swap = np.arange(HD) ^ 1
    wq_r, wk_r = arr["L0_attn_w_q_rope"], arr["L0_attn_w_k_rope"]
    wrope = np.concatenate([wq_r, wk_r, wq_r[:, swap], wk_r[:, swap]], axis=1)
    inv_freq = (1.0 / np.float32(10000.0) ** (np.arange(0, HD, 2, dtype=np.float32) / np.float32(HD))).astype(np.float32)
    ang = inv_freq[:, None] * np.arange(S, dtype=np.float32)[None, :]
    cos = np.repeat(np.cos(ang).astype(np.float32), 2, axis=0)
    sign = np.tile(np.array([-1.0, 1.0], np.float32), HD // 2)[:, None]
    sin = np.repeat(np.sin(ang).astype(np.float32), 2, axis=0) * sign
    hada = np.array([[1.0]], np.float32)
    while hada.shape[0] < 128:
        hada = np.block([[hada, hada], [hada, -hada]])
    J = 4
    order = np.arange(arr["L0_attn_w_q_up"].shape[1]).reshape(-1, J, HD).transpose(0, 2, 1).reshape(-1)
    data = {
        "x_in": arr["L0_attn_x"],
        "ct": arr["L0_c"].T,
        "wmod": arr["L0_wmod"],
        "wqd_t": arr["L0_attn_w_q_down"].T,
        "wqu": arr["L0_attn_w_q_up"][:, order],
        "wkd": arr["L0_attn_w_kv_down"],
        "wuk": arr["L0_attn_w_kv_up_k"][:, order],
        "wuv": arr["L0_attn_w_kv_up_v"],
        "wrope": wrope,
        "wout": arr["L0_attn_w_out"],
        "w1t": arr["L0_ffn_W1"].T,
        "w3t": arr["L0_ffn_W3"].T,
        "w2t": arr["L0_ffn_W2"].T,
        "cos_in": np.concatenate([cos, cos]),
        "sin_in": np.concatenate([sin, sin]),
        "ident_in": np.eye(128, dtype=np.float32),
        "hada_in": hada,
    }
    nc = bacc.Bacc("TRN2", target_bir_lowering=False, num_devices=1)
    arrays, args = {}, []
    for name, a in data.items():
        a = np.ascontiguousarray(a)
        arrays[name] = a
        args.append(nc.dram_tensor(name, a.shape, mybir.dt.from_np(a.dtype), kind="ExternalInput").ap())
    args.append(nc.dram_tensor("out", data["x_in"].shape, mybir.dt.float32, kind="ExternalOutput").ap())
    adaln_block(nc, *args)
    return run_bass_kernel_spmd(nc, [arrays], core_ids=[0]).results[0]["out"]
```

```python
import concourse.bass as bass
from concourse import mybir
from contextlib import ExitStack


def adaln_block(nc, x_in, first_in, wmod, wq_in, wb_in, w1t, w3t, w2t, trig_in, hada_in, out):
    f32 = mybir.dt.float32
    f32r = mybir.dt.float32r
    ALU = mybir.AluOpType
    ACT = mybir.ActivationFunctionType
    AX = mybir.AxisListType

    P = 128
    B, S, D = x_in.shape
    TT = S // P
    DT = D // P
    HD = trig_in.shape[0] // 4
    HEADS = D // HD
    LAT = P - trig_in.shape[0]
    HID = w1t.shape[1]
    HT = HID // P
    J = 4
    NG = HEADS // J
    STEPS = NG * TT
    LEAD = 6
    PART = 2 * HD
    MROW = 3 * PART
    SCALE = float(1.0 / (2 * HD) ** 0.5)
    EPS = 1e-5
    TILES = J * STEPS
    STACK_DMAS = 3 + 6
    LOADED = 16 * STACK_DMAS
    FW = HT * D // S

    MAXB, SCB, PVB, MA, MB = 0, 3, 5, 6, 7
    GB, UB, OB = 0, 2, 4

    ctx = ExitStack()
    sem = lambda name: ctx.enter_context(nc.semaphore(name))
    sb = lambda name, shape, dt=f32: ctx.enter_context(nc.sbuf_tensor(name, shape, dt))
    flat = lambda t: t.rearrange("p a s -> p (a s)")

    with ctx:
        ps = ctx.enter_context(nc.psum_tensor("ps", [P, 8, 512], f32))
        inv_dram = nc.dram_tensor("inv_dram", (2 * J, S), f32, kind="Internal").ap()
        gates_dram = nc.dram_tensor("gates_dram", (B, 2 * D), f32, kind="Internal").ap()

        x = sb("x", [P, B, TT, D])
        gate_now = sb("gate_now", [P, D])
        mod_t = sb("mod_t", [P, B, 8])
        stats = sb("stats", [P, TT, 6])
        mean_var = sb("mean_var", [P, TT, 2])
        var_eps, rstd = sb("var_eps", [P, TT]), sb("rstd", [P, TT])
        eps_c, half_c = sb("eps_c", [P, TT]), sb("half_c", [P, TT])
        mod_now = sb("mod_now", [P, 4])
        xn = sb("xn", [P, TT, D])
        h_raw = sb("h_raw", [P, DT, S])
        h_hi, h_lo = sb("h_hi", [P, DT, S], f32r), sb("h_lo", [P, DT, S], f32r)
        Q_LO, Q_HI, K_HI, K_LO = range(4)
        kv = sb("kv", [P, S], f32r)
        trig = sb("trig", [P, S])
        rope_c, rope_s = trig, sb("rope_s", [PART, S])
        r_hi, r_lo = sb("r_hi", [PART, S], f32r), sb("r_lo", [PART, S], f32r)
        v_new = sb("v_new", [P, TT, D])
        maxima = [sb(f"maxima{i}", [P, TT, J]) for i in range(2)]
        neg_max = sb("neg_max", [J, S], f32r)
        pv_sb = sb("pv_sb", [P, S])
        attn, inv = sb("attn", [P, DT, S]), sb("inv", [P, DT, S])
        QS = J * S // P
        sums = sb("sums", [P, 2, QS])
        attn_hi, attn_lo = sb("attn_hi", [P, DT, S], f32r), sb("attn_lo", [P, DT, S], f32r)
        first = sb("first", [P, 2 * B + P + DT * P])
        ct, ident, wkr_raw = (first[:, a:b] for a, b in ((0, 2 * B), (2 * B, 2 * B + P), (2 * B + P, 2 * B + P + DT * P)))
        silu_ct = sb("silu_ct", [P, DT, B])
        wkr_hi, wkr_lo = sb("wkr_hi", [P, DT, P], f32r), sb("wkr_lo", [P, DT, P], f32r)
        wq_hi, wq_lo = sb("wq_hi", [P, DT, D], f32r), sb("wq_lo", [P, DT, D], f32r)
        wb_hi, wb_lo = sb("wb_hi", [P, 4, D], f32r), sb("wb_lo", [P, 4, D], f32r)
        hada = sb("hada", [P, P])

        y_gated = h_raw[:, :, :].rearrange("p a (t d) -> p (a t) d", d=D)
        gate_sign, gate_row = inv[0:B, 0, :], inv[0:B, 1, :]

        def layer(*tensors):
            with ExitStack() as region:
                return [region.enter_context(nc.sbuf_tensor(*tensor)) for tensor in tensors]

        *stack, probs, parts, v_ones = layer(
            *((f"stack{g}", [P, J, 2, S], f32r) for g in range(NG)), ("probs", [P, 2, J, S], f32),
            ("parts", [P, DT, 4, S], f32r), ("v_ones", [P, TT, HEADS, HD, 2], f32))
        w2_raw, w2_mix, w3_hi, w3_lo, w1_hi, w1_lo, w2_hi, w2_lo, hid_hi, w1_raw, w3_raw, silu_sb, hid = layer(
            ("w2_raw", [P, HT, D], f32), ("w2_mix", [P, HT, D], f32),
            ("w3_hi", [P, DT, HID], f32r), ("w3_lo", [P, DT, HID], f32r),
            ("w1_hi", [P, DT, HID], f32r), ("w1_lo", [P, DT, HID], f32r),
            ("w2_hi", [P, HT, D], f32r), ("w2_lo", [P, HT, D], f32r), ("hid_hi", [P, HT, S], f32r),
            ("w1_raw", [P, DT, HID], f32), ("w3_raw", [P, DT, HID], f32),
            ("silu_sb", [P, 2, S], f32), ("hid", [P, 2, S], f32))
        _, wmod_sb, wq_raw, wb_raw, _, hid_lo = layer(
            ("places_0_to_2", [P, (NG - 1) * J * 2 * S], f32), ("wmod_sb", [P, DT, 6 * D + 2 * D], f32),
            ("wq_raw", [P, 2 * D], f32), ("wb_raw", [P, 4 * D], f32), ("rest_of_probs", [P, 2 * J * S - 6 * D], f32),
            ("hid_lo", [P, HT, S], f32r))

        first_in_sb, wmod_a, wmod_b, w_in, trig_in_sb = (sem(n) for n in ("first_in_sb", "wmod_a", "wmod_b", "w_in", "trig_in_sb"))
        x_first, x_second, x_rest = sem("x_first"), sem("x_second"), sem("x_rest")
        silu_c = sem("silu_c")
        mod_psum, mod_sb = sem("mod_psum"), sem("mod_sb")
        wq_psum, w_hi_done, w_lo_done, wq_lo_done = (sem(n) for n in ("wq_psum", "w_hi_done", "w_lo_done", "wq_lo_done"))
        gate_psum, gate_step, gate_sb, gates_sent = (sem(n) for n in ("gate_psum", "gate_step", "gate_sb", "gates_sent"))
        consts, ones_set = sem("consts"), sem("ones_set")
        stats_done, aggr_done, eps_added, rstd_done = (sem(n) for n in ("stats_done", "aggr_done", "eps_added", "rstd_done"))
        centred, xn_done, mod_copied = sem("centred"), sem("xn_done"), sem("mod_copied")
        h_ready, h_hi_done, h_lo_done = sem("h_ready"), sem("h_hi_done"), sem("h_lo_done")
        max_full, max_free = sem("max_full"), sem("max_free")
        sc_full, exp_done = sem("sc_full"), sem("exp_done")
        pv_done, pv_copied, pv_parted = sem("pv_done"), sem("pv_copied"), sem("pv_parted")
        misc_full = {b: sem(f"misc_full{b}") for b in (MA, MB)}
        kv_hi_done, kv_lo_done = sem("kv_hi_done"), sem("kv_lo_done")
        rope_mul, rope_added = sem("rope_mul"), sem("rope_added")
        rhi_done, rlo_done = sem("rhi_done"), sem("rlo_done")
        hi_done, lo_done = sem("hi_done"), sem("lo_done")
        v_evac, v_ready = sem("v_evac"), sem("v_ready")
        stack_loaded = [sem(f"stack_loaded{g}") for g in range(NG)]
        neg_ready, max_loaded = sem("neg_ready"), sem("max_loaded")
        recip_done, norm_done = sem("recip_done"), sem("norm_done")
        inv_sent, inv_loaded = sem("inv_sent"), sem("inv_loaded")
        attn_hi_done, attn_lo_done = sem("attn_hi_done"), sem("attn_lo_done")
        gate_loaded, y_gated_done, x1_done = sem("gate_loaded"), sem("y_gated_done"), sem("x1_done")
        w_loaded = [sem(f"w_loaded{i}") for i in range(3)]
        w1_split, w3_split, w2_split = sem("w1_split"), sem("w3_split"), sem("w2_split")
        w1_hi_done, w3_hi_done, w2_hi_done = sem("w1_hi_done"), sem("w3_hi_done"), sem("w2_hi_done")
        fw_scaled, fw_stage = sem("fw_scaled"), sem("fw_stage")
        gate_full, up_full, silu_done, hid_done = (sem(n) for n in ("gate_full", "up_full", "silu_done", "hid_done"))
        hid_hi_done, hid_lo_done = sem("hid_hi_done"), sem("hid_lo_done")
        t_full = sem("t_full")
        out_full, out_free, res_done, stored = (sem(n) for n in ("out_full", "out_free", "res_done", "stored"))

        MID, END = 0, 1
        TASKS = [
            (2, MID, "maxT1", MB, "cur"),
            (3, END, "hT0", MA, "ln"), (4, MID, "hT1", MB, "ln"),
            (5, END, "kvrope", MA, "nxt"),
            (6, MID, "maxT2", MB, "cur"), (6, END, "q0", MA, "nxt"),
            (7, MID, "k0", MB, "nxt"), (7, END, "q1", MA, "nxt"),
            (8, MID, "k1", MB, "nxt"),
            (9, MID, "v0", MB, "nxt"), (9, END, "v1", MA, "nxt"),
            (9, MID, "fw0", MB, "ffn"), (9, END, "fw1", MA, "ffn"),
            (10, MID, "maxT3", MB, "cur"),
            (10, END, "fw2", MA, "ffn"), (11, MID, "fw3", MB, "ffn"),
            (11, END, "out0", MA, "prev"), (12, END, "out1", MA, "prev"),
            (14, MID, "maxT0", MA, "nxt"),
        ]
        FIRST, SECOND = ("ln", "nxt"), ("cur", "ln", "nxt")
        MIDDLE, LAST = ("prev", "cur", "ln", "nxt"), ("prev", "cur", "ln", "ffn")

        class Body:

            def __init__(self, b, kinds):
                self.b, self.kinds = b, kinds
                self.prev, self.cur, self.nxt, self.ffn = (k in kinds for k in ("prev", "cur", "nxt", "ffn"))
                self.tasks = [t for t in TASKS if t[4] in kinds]

            def at(self, step, half):
                return [t[2] for t in self.tasks if t[:2] == (step, half)]

            def to_read(self, step, j):
                return {0: self.at(step - 1, END), J // 2: self.at(step, MID)}.get(j, [])

            def bank(self, name):
                return next(t[3] for t in TASKS if t[2] == name)

            def used(self, name):
                bank = self.bank(name)
                uses = lambda kinds: sum(t[3] == bank and t[4] in kinds for t in TASKS)
                here = [t[2] for t in self.tasks if t[3] == bank].index(name)
                if self.kinds == FIRST:
                    return here
                if self.kinds == SECOND:
                    return uses(FIRST) + here
                return self.b * uses(MIDDLE) + (uses(FIRST) + uses(SECOND) - uses(MIDDLE) + here)

        def bank_read(name, n):
            if name == "kvrope":
                return [(kv_lo_done, n + 1), (rope_mul, 2 * n + 2)]
            i = int(name[-1])
            if name[:2] == "fw":
                return [(fw_scaled, i + 1)]
            if name[0] in "qk":
                return [(lo_done, 4 * n + (2 * i + (name[0] == "k") + 1))]
            kind, each = {"hT": (h_ready, DT), "v": (v_evac, 2), "out": (y_gated_done, 2), "maxT": (neg_ready, NG)}[name[:-1]]
            return [(kind, each * n + i + 1)]

        def task_before(k, name):
            bank = k.bank(name)
            sequence = {"prev": k.b - 1, "cur": k.b, "nxt": k.b + 1, "ln": k.b + 1, "ffn": 0}
            here = [(t[2], sequence[t[4]]) for t in k.tasks if t[3] == bank]
            at = [t[0] for t in here].index(name)
            if at:
                return here[at - 1]
            if k.kinds == FIRST:
                return None
            kinds = {SECOND: FIRST, MIDDLE: SECOND, LAST: MIDDLE}[k.kinds]
            before = [t for t in TASKS if t[3] == bank and t[4] in kinds][-1]
            return before[2], sequence[before[4]] - 1

        def on(engine, body):
            body(Body(-1, FIRST))
            body(Body(0, SECOND))
            with engine.Fori(1, B - 1) as b:
                body(Body(b, MIDDLE))
            body(Body(B - 1, LAST))

        def on2(engine, body):
            body(0, True)
            with engine.Fori(1, B - 1) as b:
                body(b, True)
            body(B - 1, False)

        def wait(engine, semaphore, value):
            if not isinstance(value, int) or value > 0:
                engine.wait_ge(semaphore, value)

        def max_at(body, s):
            u = s + LEAD
            if u < STEPS:
                return (body.b, u // TT, u % TT) if body.cur else None
            return (body.b + 1, (u - STEPS) // TT, u % TT) if body.nxt else None

        def terms_of(a, b):
            return ((a[0], b[0]), (a[1], b[0]), (a[0], b[1]))

        transpose_at = lambda first_body: HT - 1 if first_body else 4
        TAIL_OUT_AT = 5

        block = ctx.enter_context(nc.Block())

        @block.sync
        def _(sp):
            sp.dma_start(first[:, :], first_in).then_inc(first_in_sb, 16)
            sp.dma_start(x[:, 0, :, :], x_in[0].rearrange("(t p) d -> p t d", p=P)).then_inc(x_first, 16)
            wmod_rows = wmod.rearrange("(t p) n -> p t n", p=P)
            sp.dma_start(wmod_sb[:, :, 0:2 * D], wmod_rows[:, :, 0:2 * D]).then_inc(wmod_a, 16)
            sp.dma_start(wq_raw[:, :], wq_in).then_inc(w_in, 16)
            sp.dma_start(wb_raw[:, :], wb_in).then_inc(w_in, 16)
            sp.dma_start(trig[LAT:P, :], trig_in).then_inc(trig_in_sb, 16)
            sp.dma_start(wmod_sb[:, :, 2 * D:6 * D], wmod_rows[:, :, 2 * D:6 * D]).then_inc(wmod_b, 16)
            sp.dma_start(x[:, 1, :, :], x_in[1].rearrange("(t p) d -> p t d", p=P)).then_inc(x_second, 16)
            sp.wait_ge(gate_sb, 1)
            sp.dma_start(gates_dram, gate_row).then_inc(gates_sent, 16)

            def move(to, source, signals):
                sp.dma_start(to.bitcast(f32), source.bitcast(f32)).then_inc(signals, 16)

            def load_stack(n, g, before):
                if g == 0:
                    wait(sp, rlo_done, n + 1)
                if before:
                    wait(sp, sc_full, TILES * (n - 1) + J * TT * (g + 1))
                wait(sp, lo_done, 2 * (2 * n + (g // 2 + 1)))
                rows, t = slice(J * HD * (g % 2), J * HD * (g % 2 + 1)), g // 2
                for part, (one, two) in enumerate(((Q_HI, K_HI), (Q_HI, K_LO), (Q_LO, K_HI))):
                    to = PART * part
                    move(stack[g][to:to + HD, :, :, :].rearrange("p j a s -> p (j a s)"),
                         parts[rows, t, one:two + 1:two - one, :], stack_loaded[g])
                for part, sources in enumerate(((r_hi, r_hi), (r_hi, r_lo), (r_lo, r_hi))):
                    to = PART * part + HD
                    for a, src in enumerate(sources):
                        move(stack[g][to:to + HD, :, a, :],
                             src[a * HD:(a + 1) * HD, :].rearrange("p (o s) -> p o s", o=1).to_broadcast([HD, J, S]),
                             stack_loaded[g])

            def load_max(n, g):
                wait(sp, neg_ready, NG * n + g + 1)
                move(stack[g][MROW:MROW + 1, :, 0, :], neg_max[:, :], max_loaded)

            def part_pv(n, g):
                i, rows = g // 2, slice(J * HD * (g % 2), J * HD * (g % 2 + 1))
                wait(sp, pv_copied, NG * n + g + 1)
                if g == 2:
                    wait(sp, attn_lo_done, DT * n)
                sp.dma_start(attn[rows, i, :], pv_sb[0:P:2, :]).then_inc(pv_parted, 16)
                sp.dma_start(sums[:, g % 2, :], pv_sb[1:P:2 * HD, :]).then_inc(pv_parted, 16)

            def spread_inverses(n, i):
                wait(sp, recip_done, DT * n + i + 1)
                sp.dma_start(inv_dram.rearrange("(a j) (r q) -> (j r) a q", a=2, q=QS), sums[:, :, :]).then_inc(inv_sent, 16)
                wait(sp, inv_sent, 16 * (DT * n + i + 1))
                sp.dma_start(inv[:, i, :], inv_dram.rearrange("h (o s) -> h o s", o=1)
                             .to_broadcast([2 * J, HD, S])).then_inc(inv_loaded, 16)

            def load_gate(row, which):
                sp.dma_start(gate_now[:, :], gates_dram[row, which * D:(which + 1) * D]
                             .rearrange("(o d) -> o d", o=1).to_broadcast([P, D])).then_inc(gate_loaded, 16)

            def body(k):
                if k.prev:
                    wait(sp, y_gated_done, 2 * (k.b - 1))
                    part_pv(k.b - 1, NG - 1)
                    load_gate(k.b - 1, 0)
                if k.cur:
                    load_stack(k.b, NG - 1, k.prev)
                    load_max(k.b, 1)
                if k.prev:
                    spread_inverses(k.b - 1, 1)
                if k.ffn:
                    sp.wait_ge(stack_loaded[NG - 1], LOADED * B)
                    sp.dma_start(w3_raw[:, :, :], w3t.rearrange("(t p) h -> p t h", p=P)).then_inc(w_loaded[1], 16)
                    sp.dma_start(w1_raw[:, :, :], w1t.rearrange("(t p) h -> p t h", p=P)).then_inc(w_loaded[0], 16)
                if k.cur:
                    part_pv(k.b, 0)
                    load_max(k.b, 2)
                if k.ffn:
                    sp.wait_ge(sc_full, TILES * k.b + J * TT)
                    sp.dma_start(w2_raw[:, :, :], w2t.rearrange("(t p) d -> p t d", p=P)).then_inc(w_loaded[2], 16)
                if k.nxt:
                    load_stack(k.b + 1, 0, k.cur)
                if k.cur:
                    part_pv(k.b, 1)
                if k.nxt:
                    load_stack(k.b + 1, 1, k.cur)
                if k.cur:
                    load_max(k.b, 3)
                    spread_inverses(k.b, 0)
                    part_pv(k.b, 2)
                if k.nxt:
                    load_stack(k.b + 1, 2, k.cur)
                if k.cur:
                    wait(sp, attn_lo_done, DT * k.b + 1)
                if k.nxt:
                    load_max(k.b + 1, 0)
                if not k.cur:
                    for b in range(2, B):
                        sp.dma_start(x[:, b, :, :], x_in[b].rearrange("(t p) d -> p t d", p=P)).then_inc(x_rest, 16)
                    sp.dma_start(hada[:, :], hada_in).then_inc(x_rest, 16)
                    sp.wait_ge(gates_sent, 16)

            on(sp, body)

            sp.wait_ge(y_gated_done, 2 * (B - 1))
            part_pv(B - 1, NG - 1)
            load_gate(B - 1, 0)
            spread_inverses(B - 1, 1)

            sp.wait_ge(y_gated_done, 2 * B)
            for b in range(B):
                wait(sp, out_free, TT * b)
                load_gate(b, 1)
                sp.wait_ge(res_done, TT * (b + 1))
                sp.dma_start(out[b].rearrange("(t p) d -> p t d", p=P), x[:, b, :, :]).then_inc(stored, 16)
            sp.wait_ge(stored, 16 * B)

        @block.tensor
        def _(pe):
            def modulation(bank, chunks):
                for i, chunk in enumerate(chunks):
                    for t in range(DT):
                        col = chunk * D + t * P
                        for kt in range(DT):
                            last = nc.tensor.matmul(ps[:, bank, (i * DT + t) * B:(i * DT + t + 1) * B],
                                                    wmod_sb[:, kt, col:col + P], silu_ct[:, kt, :],
                                                    start=kt == 0, stop=kt == DT - 1)
                last.then_inc(mod_psum, 1)

            pe.wait_ge(silu_c, 1)
            pe.wait_ge(wmod_a, 16)
            modulation(MA, (0, 1))
            pe.wait_ge(w_in, 32)
            for t in range(DT):
                last = nc.tensor.matmul(ps[:, PVB, t * D:(t + 1) * D], wq_raw[:, t * P:(t + 1) * P],
                                        wq_raw[:, D:2 * D], start=True, stop=True)
            last.then_inc(wq_psum, 1)
            pe.wait_ge(wmod_b, 16)
            modulation(SCB, (3, 4))
            for i, chunk in enumerate((2, 5)):
                for kt in range(DT):
                    last = nc.tensor.matmul(ps[0:B, SCB + 1, i * D:(i + 1) * D], silu_ct[:, kt, :],
                                            wmod_sb[:, kt, chunk * D:(chunk + 1) * D],
                                            start=kt == 0, stop=kt == DT - 1)
            last.then_inc(gate_psum, 1)

            def product(dst, pairs, n_terms, start=True):
                for i, (a, b) in enumerate(pairs):
                    last = nc.tensor.matmul(dst, a, b, start=start and i == 0, stop=i == n_terms - 1)
                return last

            def transposed(bank, n):
                for t in range(TT):
                    last = nc.tensor.transpose(ps[:, bank, t * P:(t + 1) * P], xn[:, t, n * P:(n + 1) * P], ident)
                return last

            def project_out(bank, n):
                for i in range(2):
                    tokens = slice((2 * n + i) * P, (2 * n + i + 1) * P)
                    pairs = [(a[:, kt, tokens], w[:, 2 + kt, :])
                             for a, w in terms_of((attn_hi, attn_lo), (wb_hi, wb_lo)) for kt in range(DT)]
                    last = product(ps[:, bank, i * D:(i + 1) * D], pairs, len(pairs))
                return last

            def prob_v(b, s):
                pg, pt = divmod(s, TT)
                wait(pe, exp_done, TILES * b + J * (s + 1))
                if pt == 0:
                    wait(pe, v_ready, NG * b + pg + 1)
                    wait(pe, pv_copied, NG * b + pg)
                for j in range(J):
                    last = nc.tensor.matmul(ps[2 * HD * j:2 * HD * (j + 1), PVB, :],
                                            v_ones[:, pt, J * pg + j, :, :].rearrange("p d o -> p (d o)"),
                                            probs[:, s % 2, j, :], start=pt == 0, stop=pt == TT - 1)
                last.then_inc(pv_done, 1)

            def task(k, name):
                bank = k.bank(name)
                before = task_before(k, name)
                if before:
                    for semaphore, count in bank_read(*before):
                        wait(pe, semaphore, count)
                n = int(name[-1]) if name[-1].isdigit() else 0
                if name[:2] == "hT":
                    wait(pe, xn_done, 2 * (k.b + 2))
                    last = transposed(bank, n)
                elif name == "kvrope":
                    wait(pe, h_hi_done, DT * (k.b + 2))
                    wait(pe, h_lo_done, DT * (k.b + 2))
                    pairs = [(w[:, t, :], h[:, t, :]) for w, h in terms_of((wkr_hi, wkr_lo), (h_hi, h_lo)) for t in range(DT)]
                    last = product(ps[:, bank, :], pairs, len(pairs))
                elif name[0] == "q":
                    pairs = [(w[:, t, n * P:(n + 1) * P], h[:, t, :])
                             for w, h in terms_of((wq_hi, wq_lo), (h_hi, h_lo)) for t in range(DT)]
                    last = product(ps[:, bank, :], pairs, len(pairs))
                elif name[0] == "k":
                    wait(pe, kv_lo_done, k.b + 2)
                    cols = slice(n * P, (n + 1) * P)
                    last = product(ps[:, bank, :], [(wb_hi[:, 0, cols], kv[:, :]), (wb_lo[0:LAT, 0, cols], kv[0:LAT, :])], 2)
                elif name[0] == "v":
                    for i in range(2):
                        tokens = slice((2 * n + i) * P, (2 * n + i + 1) * P)
                        last = product(ps[:, bank, i * D:(i + 1) * D],
                                       [(kv[:, tokens], wb_hi[:, 1, :]), (kv[0:LAT, tokens], wb_lo[0:LAT, 1, :])], 2)
                elif name[:4] == "maxT":
                    nb = k.b + 1 if n == 0 else k.b
                    wait(pe, max_free, TILES * nb + J * TT * (n + 1))
                    for t in range(TT):
                        last = nc.tensor.transpose(ps[0:J, bank, t * P:(t + 1) * P], maxima[n % 2][:, t, :], ident)
                elif name[:2] == "fw":
                    pe.wait_ge(w_loaded[2], 16)
                    last = nc.tensor.matmul(ps[:, bank, :], hada[:, :], w2_raw[:, :, :].rearrange("p t d -> p (t d)")[:, n * S:(n + 1) * S],
                                            start=True, stop=True)
                else:
                    wait(pe, attn_lo_done, DT * k.b)
                    last = project_out(bank, n)
                last.then_inc(misc_full[bank], 1)

            def body(k):
                if k.kinds == SECOND:
                    pe.wait_ge(ones_set, NG)
                for s in range(STEPS):
                    g, kt = divmod(s, TT)
                    ahead = max_at(k, s)

                    def max_tile(j):
                        n, mg, qt = ahead
                        if qt == 0 and j == 0:
                            wait(pe, stack_loaded[mg], LOADED * (n + 1))
                        at = J * (TT * mg + qt) + j
                        tile = TILES * n + at
                        wait(pe, max_free, tile - 2 if at >= 3 else tile if at == 0 else tile - 3)
                        nc.tensor.matmul(ps[:, MAXB + at % 3, :], stack[mg][0:MROW, j, 0, qt * P:(qt + 1) * P],
                                         stack[mg][0:MROW, j, 1, :], start=True, stop=True).then_inc(max_full, 1)

                    def score_tile(j):
                        if kt == 0 and j == 0:
                            wait(pe, max_loaded, 16 * (NG * k.b + g + 1))
                        tile = TILES * k.b + J * s + j
                        wait(pe, exp_done, tile - 1)
                        nc.tensor.matmul(ps[:, SCB + j % 2, :], stack[g][0:MROW + 1, j, 1, kt * P:(kt + 1) * P],
                                         stack[g][0:MROW + 1, j, 0, :], start=True, stop=True).then_inc(sc_full, 1)

                    for half in (0, 2):
                        for j in (half, half + 1):
                            if ahead:
                                max_tile(j)
                            if k.cur:
                                score_tile(j)
                        if half == 0 and s > 0 and k.cur:
                            prob_v(k.b, s - 1)
                        if half == 0 and s == 0 and k.prev:
                            prob_v(k.b - 1, STEPS - 1)
                        for name in k.at(s, MID if half == 0 else END):
                            task(k, name)

            pe.wait_ge(consts, 1)
            pe.wait_ge(mod_sb, 4)
            pe.wait_ge(gate_sb, 1)
            pe.wait_ge(w_hi_done, 3)
            pe.wait_ge(w_lo_done, 2)
            pe.wait_ge(wq_lo_done, 1)
            on(pe, body)

            def body2(b, nxt):
                n = b + B
                wait(pe, h_hi_done, DT * (n + 1))
                wait(pe, h_lo_done, DT * (n + 1))
                first_body = isinstance(b, int) and b == 0
                for m in range(HT):
                    cols = slice(m * P, (m + 1) * P)
                    for bank, full, read, (w_hi, w_lo), split in (
                            (GB, gate_full, silu_done, (w1_hi, w1_lo), w1_split),
                            (UB, up_full, hid_done, (w3_hi, w3_lo), w3_split)):
                        if first_body and m == 0:
                            pe.wait_ge(split, DT)
                        wait(pe, read, HT * b + m - 1)
                        pairs = [(w[:, kt, cols], h[:, kt, :])
                                 for w, h in terms_of((w_hi, w_lo), (h_hi, h_lo)) for kt in range(DT)]
                        product(ps[:, bank + m % 2, :], pairs, len(pairs)).then_inc(full, 1)
                        if first_body and m == 0 and bank == GB:
                            prob_v(B - 1, STEPS - 1)
                    if first_body and m == TAIL_OUT_AT:
                        pe.wait_ge(attn_lo_done, DT * B)
                        pe.wait_ge(neg_ready, NG * B)
                        pe.wait_ge(y_gated_done, 2 * (B - 1))
                        pe.wait_ge(fw_scaled, FW)
                        for i, bank in enumerate((MA, MB)):
                            project_out(bank, i).then_inc(misc_full[bank], 1)
                    if m == transpose_at(first_body) and nxt:
                        wait(pe, out_free, TT * b)
                        if first_body:
                            pe.wait_ge(pv_copied, NG * B)
                        wait(pe, xn_done, 2 * (n + 2))
                        for t2 in range(DT):
                            transposed(OB + t2, t2).then_inc(t_full, 1)
                if first_body:
                    pe.wait_ge(y_gated_done, 2 * B)
                    pe.wait_ge(w2_split, DT)
                wait(pe, h_ready, DT * (n + 2) if nxt else DT * (n + 1))
                wait(pe, out_free, TT * b)
                for m in range(HT):
                    wait(pe, hid_hi_done, HT * b + m + 1)
                    wait(pe, hid_lo_done, HT * b + m + 1)
                    for t in range(TT):
                        rows = slice(t * P, (t + 1) * P)
                        for i, (h, w) in enumerate(terms_of((hid_hi, hid_lo), (w2_hi, w2_lo))):
                            last = nc.tensor.matmul(ps[:, OB + t, 0:D], h[:, m, rows], w[:, m, :],
                                                    start=m == 0 and i == 0, stop=m == HT - 1 and i == 2)
                        if m == HT - 1:
                            last.then_inc(out_full, 1)

            on2(pe, body2)

        @block.scalar
        def _(act):
            act.wait_ge(first_in_sb, 16)
            nc.scalar.activation(silu_ct[:, :, :].rearrange("p t b -> p (t b)"), ct, ACT.Silu).then_inc(silu_c, 1)
            nc.scalar.copy(flat(wkr_hi[:, :, :]), wkr_raw).then_inc(w_hi_done, 1)
            act.wait_ge(w_in, 32)
            nc.scalar.copy(flat(wb_hi[:, :, :]), wb_raw[:, :]).then_inc(w_hi_done, 1)
            act.wait_ge(wq_psum, 1)
            nc.scalar.copy(flat(wq_hi[:, :, :]), ps[:, PVB, :]).then_inc(w_hi_done, 1)

            def modulate(n, i, bank):
                if i == 0:
                    wait(act, mod_copied, n + 1)
                nc.scalar.activation(h_raw[:, i, :], ps[:, bank, :], ACT.Identity,
                                     scale=mod_now[:, 2 + i:3 + i], bias=mod_now[:, i:i + 1]).then_inc(h_ready, 1)

            def h_hi_part(n, i):
                wait(act, h_ready, DT * n + i + 1)
                nc.scalar.copy(h_hi[:, i, :], h_raw[:, i, :]).then_inc(h_hi_done, 1)

            def copy_pv(n, g):
                wait(act, pv_done, STEPS * n + TT * (g + 1))
                wait(act, pv_parted, 32 * (NG * n + g))
                nc.scalar.copy(pv_sb[:, :], ps[:, PVB, :]).then_inc(pv_copied, 1)

            def attn_hi_part(n, i):
                wait(act, norm_done, DT * n + i + 1)
                wait(act, y_gated_done, 2 * n)
                nc.scalar.copy(attn_hi[:, i, :], attn[:, i, :]).then_inc(attn_hi_done, 1)

            def body(k):
                for s in range(STEPS):
                    for j in range(J):
                        if s % TT == 0 and j == J // 2:
                            if s == 0 and k.prev:
                                copy_pv(k.b - 1, NG - 1)
                            elif s and k.cur:
                                copy_pv(k.b, s // TT - 1)
                        if (s, j) == (8, 0) and k.prev:
                            attn_hi_part(k.b - 1, 1)
                        if (s, j) == (13, 2) and k.cur:
                            attn_hi_part(k.b, 0)
                        for name in k.to_read(s, j):
                            read_task(k, name)
                        if s == 4 and j % 2 == 1:
                            h_hi_part(k.b + 1, j // 2)
                        if k.cur:
                            exponentials(k, s, j)
                        if k.ffn and j == J - 1:
                            split_weights(k, s)

            def exponentials(k, s, j):
                wait(act, sc_full, TILES * k.b + J * s + j + 1)
                if j == 0:
                    wait(act, pv_done, STEPS * k.b + s - 1)
                nc.scalar.activation(probs[:, s % 2, j, :], ps[:, SCB + j % 2, :], ACT.Exp, scale=SCALE).then_inc(exp_done, 1)

            def split_weights(k, s):
                for at, loaded, done, hi, raw, g in ((8, w_loaded[1], w3_hi_done, w3_hi, w3_raw, 1),
                                                     (12, w_loaded[0], w1_hi_done, w1_hi, w1_raw, 2)):
                    if s in (at, at + 1):
                        if s == at:
                            act.wait_ge(loaded, 16)
                            act.wait_ge(sc_full, TILES * k.b + J * TT * (g + 1))
                        nc.scalar.copy(hi[:, s - at, :], raw[:, s - at, :]).then_inc(done, 1)

            def read_task(k, name):
                bank = k.bank(name)
                n = int(name[-1]) if name[-1].isdigit() else 0
                if name[:2] == "hT":
                    if n == 0:
                        wait(act, x1_done, 2 * (k.b - 1))
                        wait(act, h_lo_done, DT * (k.b + 1))
                        wait(act, lo_done, 4 * (k.b + 1))
                    wait(act, misc_full[bank], k.used(name) + 1)
                    modulate(k.b + 1, n, bank)
                elif name == "kvrope":
                    wait(act, v_evac, 2 * (k.b + 1))
                    wait(act, misc_full[bank], k.used(name) + 1)
                    nc.scalar.copy(kv[0:LAT, :], ps[0:LAT, bank, :]).then_inc(kv_hi_done, 1)
                elif name[0] in "qk":
                    wait(act, stack_loaded[2 * n + 1], LOADED * (k.b + 1))
                    wait(act, misc_full[bank], k.used(name) + 1)
                    nc.scalar.copy(parts[:, n, Q_HI if name[0] == "q" else K_HI, :], ps[:, bank, :]).then_inc(hi_done, 1)
                elif name[0] == "v":
                    wait(act, v_ready, NG * (k.b + 1))
                    wait(act, misc_full[bank], k.used(name) + 1)
                    nc.scalar.copy(v_new[:, 2 * n:2 * n + 2, :], ps[:, bank, :].rearrange("p (t d) -> p t d", t=2)).then_inc(v_evac, 1)
                elif name[:4] == "maxT":
                    nb = k.b + 1 if n == 0 else k.b
                    wait(act, max_loaded, 16 * (NG * nb + n))
                    wait(act, misc_full[bank], k.used(name) + 1)
                    nc.scalar.activation(neg_max[:, :], ps[0:J, bank, :], ACT.Copy, scale=-1.0).then_inc(neg_ready, 1)
                elif name[:2] == "fw":
                    wait(act, misc_full[bank], k.used(name) + 1)
                    nc.scalar.activation(w2_mix[:, :, :].rearrange("p t d -> p (t d)")[:, n * S:(n + 1) * S],
                                         ps[:, bank, :], ACT.Copy, scale=float(HID ** -0.5)).then_inc(fw_scaled, 1)

            on(act, body)

            copy_pv(B - 1, NG - 1)

            def body2(b, nxt):
                first_body = isinstance(b, int) and b == 0
                for m in range(HT + 1):
                    if m < HT:
                        wait(act, gate_full, HT * b + m + 1)
                        wait(act, hid_done, HT * b + m - 1)
                        nc.scalar.activation(silu_sb[:, m % 2, :], ps[:, GB + m % 2, :], ACT.Silu).then_inc(silu_done, 1)
                    if m >= 1:
                        wait(act, hid_done, HT * b + m)
                        nc.scalar.copy(hid_hi[:, m - 1, :], hid[:, (m - 1) % 2, :]).then_inc(hid_hi_done, 1)
                    if first_body and m == TAIL_OUT_AT - 1:
                        attn_hi_part(B - 1, 1)
                    if first_body and m in (1, 2):
                        half = slice((m - 1) * HT // 2, m * HT // 2)
                        act.wait_ge(fw_stage, 6)
                        nc.scalar.copy(w2_hi[:, half, :], w2_raw[:, half, :]).then_inc(w2_hi_done, 1)
                    if m == transpose_at(first_body) + 1 and nxt:
                        n = b + (B + 1)
                        if first_body:
                            act.wait_ge(x1_done, 2 * B)
                        else:
                            act.wait_ge(res_done, TT * b)
                        for i in range(DT):
                            wait(act, t_full, DT * b + i + 1)
                            modulate(n, i, OB + i)
                if nxt:
                    n = b + (B + 1)
                    wait(act, up_full, HT * b + HT)
                    for i in range(DT):
                        h_hi_part(n, i)
            on2(act, body2)

        @block.vector
        def _(dve):
            def statistics(n, at, t):
                nc.vector.bn_stats(stats[:, t, :], x[:, at, t, :]).then_inc(stats_done, 1)

            def aggregates(n, n_mod=None):
                wait(dve, stats_done, TT * (n + 1))
                if n_mod is not None:
                    at, part = n_mod
                    nc.vector.tensor_copy(mod_now[:, :], mod_t[:, at, 4 * part:4 * part + 4]).then_inc(mod_copied, 1)
                for t in range(TT):
                    nc.vector.bn_aggr(mean_var[:, t, :], stats[:, t, :]).then_inc(aggr_done, 1)

            nc.vector.memset(eps_c[:, :], EPS)
            nc.vector.memset(half_c[:, :], -0.5).then_inc(consts, 1)
            for g in range(2):
                nc.vector.memset(stack[g][MROW:MROW + 1, :, 1, :].bitcast(f32), 1.0).then_inc(ones_set, 1)
            dve.wait_ge(x_first, 16)
            for t in range(TT):
                statistics(0, 0, t)
            aggregates(0)
            for half, bank in enumerate((MA, SCB)):
                dve.wait_ge(mod_psum, half + 1)
                modp = ps[:, bank, 0:4 * B].rearrange("p (i b) -> p b i", b=B)
                for i in range(2):
                    nc.vector.tensor_scalar(mod_t[:, :, 4 * half + 2 * i:4 * half + 2 * i + 2], modp[:, :, 2 * i:2 * i + 2],
                                            float(i), None, ALU.add).then_inc(mod_sb, 1)
                if half == 0:
                    dve.wait_ge(mod_sb, 2)
                    nc.vector.tensor_copy(mod_now[:, :], mod_t[:, 0, 0:4]).then_inc(mod_copied, 1)
                    dve.wait_ge(rstd_done, 1)
                    for t in range(TT):
                        last = nc.vector.tensor_scalar(xn[:, t, :], x[:, 0, t, :], mean_var[:, t, 0:1],
                                                       rstd[:, t:t + 1], ALU.subtract, ALU.mult)
                        if t % 2:
                            last.then_inc(xn_done, 1)
                    dve.wait_ge(w_hi_done, 3)
                    nc.vector.tensor_tensor(flat(wq_lo[:, :, :]), ps[:, PVB, :], flat(wq_hi[:, :, :]).bitcast(f32), ALU.subtract).then_inc(wq_lo_done, 1)
            dve.wait_ge(gate_psum, 1)
            gate_in = ps[0:B, SCB + 1, :]
            nc.vector.tensor_scalar(gate_sign, gate_in, 0.0, 2.0, ALU.is_ge, ALU.mult).then_inc(gate_step, 1)
            dve.wait_ge(gate_step, 1)
            nc.vector.tensor_scalar(gate_sign, gate_sign, -1.0, None, ALU.add).then_inc(gate_step, 1)
            dve.wait_ge(gate_step, 2)
            nc.vector.tensor_tensor(gate_row, gate_in, gate_sign, ALU.mult).then_inc(gate_step, 1)
            dve.wait_ge(gate_step, 3)
            nc.vector.scalar_tensor_tensor(out=gate_row, in0=gate_row, scalar=0.25, in1=gate_sign,
                                           op0=ALU.max, op1=ALU.mult).then_inc(gate_sb, 1)
            for g in (2, 3):
                nc.vector.memset(stack[g][MROW:MROW + 1, :, 1, :].bitcast(f32), 1.0).then_inc(ones_set, 1)

            def layer_norm(n, at, part, s, j):
                if s == 0:
                    if j == 0:
                        wait(dve, h_ready, DT * n)
                    statistics(n, at, j)
                elif s == 1 and j == 0:
                    aggregates(n, (at, part))

            def invert_sums(n, i):
                wait(dve, pv_parted, 32 * (NG * n + 2 * i + 2))
                nc.vector.reciprocal(sums[:, :, :], sums[:, :, :]).then_inc(recip_done, 1)

            def normalise_attn(n, i):
                wait(dve, inv_loaded, 16 * (DT * n + i + 1))
                nc.vector.tensor_tensor(attn[:, i, :], attn[:, i, :], inv[:, i, :], ALU.mult).then_inc(norm_done, 1)

            def gate_attn(n, i, bank):
                if i == 0:
                    wait(dve, gate_loaded, 16 * (n + 1))
                ga = gate_now[:, :].rearrange("p (o d) -> p o d", o=1).to_broadcast([P, 2, D])
                nc.vector.tensor_tensor(y_gated[:, 2 * i:2 * i + 2, :], ps[:, bank, :].rearrange("p (t d) -> p t d", t=2),
                                        ga, ALU.mult).then_inc(y_gated_done, 1)

            def body(k):
                for s in range(STEPS):
                    for j in range(J):
                        for name in k.to_read(s, j):
                            read_task(k, name)
                        if max_at(k, s):
                            reduce_max(*max_at(k, s), j)
                        if k.nxt and k.cur:
                            if k.kinds == SECOND and (s, j) == (0, 0):
                                dve.wait_ge(x_second, 16)
                                dve.wait_ge(x_rest, 16 * (B - 1))
                            layer_norm(k.b + 1, k.b + 1, 0, s, j)
                        if k.ffn:
                            layer_norm(B, 0, 1, s, j)
                        if (s, j) == (2, 0) and k.prev:
                            invert_sums(k.b - 1, 1)
                        if (s, j) == (7, 0) and k.prev:
                            normalise_attn(k.b - 1, 1)
                        if (s, j) == (10, 0) and k.cur:
                            invert_sums(k.b, 0)
                        if (s, j) == (12, 2) and k.cur:
                            normalise_attn(k.b, 0)
                    if k.ffn:
                        prepare_weights(s)

            def prepare_weights(s):
                if s in (12, 13, 14):
                    stage = s - 12
                    h = 1 << stage
                    src, dst = (w2_mix, w2_raw) if stage % 2 == 0 else (w2_raw, w2_mix)
                    a, c = (v[:, :, :].rearrange("p (n two h) d -> p n two (h d)", two=2, h=h) for v in (src, dst))
                    dve.wait_ge(*((fw_stage, 2 * stage) if stage else (fw_scaled, FW)))
                    nc.vector.tensor_tensor(c[:, :, 0, :], a[:, :, 0, :], a[:, :, 1, :], ALU.add).then_inc(fw_stage, 1)
                    nc.vector.tensor_tensor(c[:, :, 1, :], a[:, :, 0, :], a[:, :, 1, :], ALU.subtract).then_inc(fw_stage, 1)
                if s in (13, 14):
                    dve.wait_ge(w1_hi_done, s - 12)
                    nc.vector.tensor_tensor(w1_lo[:, s - 13, :], w1_raw[:, s - 13, :], w1_hi[:, s - 13, :].bitcast(f32), ALU.subtract).then_inc(w1_split, 1)

            def reduce_max(n, mg, qt, j):
                at = J * (TT * mg + qt) + j
                wait(dve, max_full, TILES * n + at + 1)
                nc.vector.tensor_reduce(out=maxima[mg % 2][:, qt, j:j + 1], in_=ps[:, MAXB + at % 3, :],
                                        axis=AX.X, op=ALU.max).then_inc(max_free, 1)

            def read_task(k, name):
                bank = k.bank(name)
                n = int(name[-1]) if name[-1].isdigit() else 0
                if name == "kvrope":
                    wait(dve, rlo_done, k.b + 1)
                    wait(dve, misc_full[bank], k.used(name) + 1)
                    if k.kinds == FIRST:
                        dve.wait_ge(trig_in_sb, 16)
                    nc.vector.tensor_tensor(rope_c[0:PART, :], ps[LAT:LAT + PART, bank, :], trig[LAT:LAT + PART, :], ALU.mult).then_inc(rope_mul, 1)
                    nc.vector.tensor_tensor(rope_s[:, :], ps[LAT + PART:P, bank, :], trig[LAT + PART:P, :], ALU.mult).then_inc(rope_mul, 1)
                    wait(dve, kv_hi_done, k.b + 2)
                    nc.vector.tensor_tensor(kv[LAT:P, :], ps[0:LAT, bank, :], kv[0:LAT, :].bitcast(f32), ALU.subtract).then_inc(kv_lo_done, 1)
                elif name[:3] == "out":
                    wait(dve, misc_full[bank], k.used(name) + 1)
                    if n == 0:
                        wait(dve, h_lo_done, DT * (k.b + 2))
                    gate_attn(k.b - 1, n, bank)
                elif name[0] in "qk":
                    order = 2 * n + (name[0] == "k")
                    hi, lo = (parts[:, n, i, :] for i in ((Q_HI, Q_LO) if name[0] == "q" else (K_HI, K_LO)))
                    wait(dve, stack_loaded[2 * n + 1], LOADED * (k.b + 1))
                    wait(dve, hi_done, 4 * (k.b + 1) + order + 1)
                    nc.vector.tensor_tensor(lo, ps[:, bank, :], hi.bitcast(f32), ALU.subtract).then_inc(lo_done, 1)

            on(dve, body)

            def body2(b, nxt):
                first_body = isinstance(b, int) and b == 0
                for m in range(HT + 1):
                    if m < HT:
                        wait(dve, silu_done, HT * b + m + 1)
                        wait(dve, up_full, HT * b + m + 1)
                        wait(dve, hid_lo_done, HT * b + m - 1)
                        nc.vector.tensor_tensor(hid[:, m % 2, :], ps[:, UB + m % 2, :], silu_sb[:, m % 2, :], ALU.mult).then_inc(hid_done, 1)
                    if m >= 1:
                        wait(dve, hid_hi_done, HT * b + m)
                        nc.vector.tensor_tensor(hid_lo[:, m - 1, :], hid[:, (m - 1) % 2, :],
                                                hid_hi[:, m - 1, :].bitcast(f32), ALU.subtract).then_inc(hid_lo_done, 1)
                    if first_body and m == 1:
                        invert_sums(B - 1, 1)
                    if first_body and m == TAIL_OUT_AT - 1:
                        normalise_attn(B - 1, 1)
                    if first_body and m == TAIL_OUT_AT + 1:
                        for i, bank in enumerate((MA, MB)):
                            tasks = sum(t[3] == bank and t[4] in kinds for t in TASKS
                                        for kinds in (FIRST, SECOND, LAST) + (MIDDLE,) * (B - 2))
                            dve.wait_ge(misc_full[bank], tasks + 1)
                            gate_attn(B - 1, i, bank)
                    if nxt and m == 0:
                        if not first_body:
                            dve.wait_ge(x1_done, 2 * B)
                        for j in range(TT):
                            layer_norm(b + (B + 1), b + 1, 1, 0, j)
                        layer_norm(b + (B + 1), b + 1, 1, 1, 0)
                for t in range(TT):
                    wait(dve, out_full, TT * b + t + 1)
                    if t == 0:
                        wait(dve, res_done, TT * b)
                        wait(dve, gate_loaded, 16 * (B + b + 1))
                        if nxt:
                            wait(dve, h_lo_done, DT * (b + (B + 2)))
                    nc.vector.tensor_tensor(y_gated[:, t, :], ps[:, OB + t, 0:D], gate_now[:, :], ALU.mult).then_inc(out_free, 1)
            on2(dve, body2)

        @block.gpsimd
        def _(pool):
            nc.gpsimd.memset(v_ones[:, :, :, :, :], 1.0).then_inc(consts, 1)
            pool.wait_ge(consts, 2)

            def deviation(n):
                wait(pool, aggr_done, TT * (n + 1))
                wait(pool, xn_done, 2 * n)
                nc.gpsimd.tensor_tensor(var_eps[:, :], mean_var[:, :, 1], eps_c[:, :], ALU.add).then_inc(eps_added, 1)
                wait(pool, eps_added, n + 1)
                nc.gpsimd.tensor_tensor(rstd[:, :], var_eps[:, :], half_c[:, :], ALU.pow).then_inc(rstd_done, 1)

            def normalise(n, at):
                wait(pool, rstd_done, n + 1)
                for i in range(2):
                    tiles = slice(2 * i, 2 * i + 2)
                    nc.gpsimd.tensor_tensor(xn[:, tiles, :], x[:, at, tiles, :],
                                            mean_var[:, tiles, 0:1].to_broadcast([P, 2, D]), ALU.subtract).then_inc(centred, 1)
                    wait(pool, centred, 2 * (n - 1) + (i + 1))
                    nc.gpsimd.tensor_tensor(xn[:, tiles, :], xn[:, tiles, :],
                                            rstd[:, tiles].rearrange("p (t o) -> p t o", o=1).to_broadcast([P, 2, D]), ALU.mult).then_inc(xn_done, 1)

            def h_lo_parts(n):
                for i in range(DT):
                    wait(pool, h_hi_done, DT * n + i + 1)
                    nc.gpsimd.tensor_tensor(h_lo[:, i, :], h_raw[:, i, :], h_hi[:, i, :].bitcast(f32), ALU.subtract).then_inc(h_lo_done, 1)

            def attn_lo_part(n, i):
                wait(pool, attn_hi_done, DT * n + i + 1)
                wait(pool, y_gated_done, 2 * n)
                nc.gpsimd.tensor_tensor(attn_lo[:, i, :], attn[:, i, :], attn_hi[:, i, :].bitcast(f32), ALU.subtract).then_inc(attn_lo_done, 1)

            def add_attention(n, i):
                wait(pool, y_gated_done, 2 * n + i + 1)
                here = x[:, n, 2 * i:2 * i + 2, :]
                nc.gpsimd.tensor_tensor(here, here, y_gated[:, 2 * i:2 * i + 2, :], ALU.add).then_inc(x1_done, 1)

            deviation(0)
            for i, (lo, raw, hi) in enumerate(((wkr_lo, wkr_raw, wkr_hi), (wb_lo, wb_raw[:, :], wb_hi))):
                pool.wait_ge(w_hi_done, i + 1)
                nc.gpsimd.tensor_tensor(flat(lo[:, :, :]), raw, flat(hi[:, :, :]).bitcast(f32), ALU.subtract).then_inc(w_lo_done, 1)

            def copy_v(n, g, waits):
                wait(pool, v_evac, 2 * (n + 1))
                if waits:
                    wait(pool, pv_done, STEPS * (n - 1) + TT * (g + 1))
                new = v_new[:, :, J * HD * g:J * HD * (g + 1)].rearrange("p t (j d) -> p t j d", j=J)
                place = v_ones[:, :, J * g:J * (g + 1), :, :]
                nc.gpsimd.tensor_tensor(place[:, :, :, :, 0], new, place[:, :, :, :, 1], ALU.mult).then_inc(v_ready, 1)

            def body(k):
                if k.cur:
                    copy_v(k.b, NG - 1, k.prev)
                if k.kinds != FIRST:
                    n = k.b + 1
                    deviation(n)
                    normalise(n, 0 if k.ffn else n)
                h_lo_parts(k.b + 1)
                if k.nxt:
                    wait(pool, stack_loaded[NG - 1], LOADED * (k.b + 1))
                    wait(pool, rope_mul, 2 * (k.b + 2))
                    turned = rope_c[0:PART, :]
                    nc.gpsimd.tensor_tensor(r_hi[:, :], turned, rope_s[:, :], ALU.add).then_inc(rhi_done, 1)
                    wait(pool, rhi_done, k.b + 2)
                    nc.gpsimd.tensor_tensor(turned, turned, rope_s[:, :], ALU.add).then_inc(rope_added, 1)
                    wait(pool, rope_added, k.b + 2)
                    nc.gpsimd.tensor_tensor(r_lo[:, :], turned, r_hi[:, :].bitcast(f32), ALU.subtract).then_inc(rlo_done, 1)
                    for g in range(2):
                        copy_v(k.b + 1, g, k.cur)
                if k.ffn:
                    for i in range(DT):
                        pool.wait_ge(w3_hi_done, i + 1)
                        nc.gpsimd.tensor_tensor(w3_lo[:, i, :], w3_raw[:, i, :], w3_hi[:, i, :].bitcast(f32), ALU.subtract).then_inc(w3_split, 1)
                if k.prev:
                    attn_lo_part(k.b - 1, 1)
                    for i in range(2):
                        add_attention(k.b - 1, i)
                if k.nxt:
                    copy_v(k.b + 1, 2, k.cur)
                if k.cur:
                    attn_lo_part(k.b, 0)

            on(pool, body)

            def body2(b, nxt):
                first_body = isinstance(b, int) and b == 0
                n = b + (B + 1)
                if nxt:
                    deviation(n)
                    normalise(n, b + 1)
                if first_body:
                    for i in range(2):
                        pool.wait_ge(w2_hi_done, i + 1)
                        half = slice(i * HT // 2, (i + 1) * HT // 2)
                        nc.gpsimd.tensor_tensor(w2_lo[:, half, :], w2_raw[:, half, :], w2_hi[:, half, :].bitcast(f32), ALU.subtract).then_inc(w2_split, 1)
                    attn_lo_part(B - 1, 1)
                    for i in range(2):
                        add_attention(B - 1, i)
                if nxt:
                    wait(pool, up_full, HT * b + HT)
                    h_lo_parts(n)
                for t in range(TT):
                    wait(pool, out_free, TT * b + t + 1)
                    here = x[:, b, t, :]
                    nc.gpsimd.tensor_tensor(here, here, y_gated[:, t, :], ALU.add).then_inc(res_done, 1)
            on2(pool, body2)


def kernel(**inputs):
    import numpy as np
    import concourse.bacc as bacc
    from concourse.bass_utils import run_bass_kernel_spmd

    arr = {n: np.ascontiguousarray(v) for n, v in inputs.items()}
    S, HD = arr["L0_attn_x"].shape[1], arr["L0_attn_w_k_rope"].shape[1]
    swap = np.arange(HD) ^ 1
    wq_r, wk_r = arr["L0_attn_w_q_rope"], arr["L0_attn_w_k_rope"]
    wrope = np.concatenate([wq_r, wk_r, wq_r[:, swap], wk_r[:, swap]], axis=1)
    inv_freq = (1.0 / np.float32(10000.0) ** (np.arange(0, HD, 2, dtype=np.float32) / np.float32(HD))).astype(np.float32)
    ang = inv_freq[:, None] * np.arange(S, dtype=np.float32)[None, :]
    cos = np.repeat(np.cos(ang).astype(np.float32), 2, axis=0)
    sign = np.tile(np.array([-1.0, 1.0], np.float32), HD // 2)[:, None]
    sin = np.repeat(np.sin(ang).astype(np.float32), 2, axis=0) * sign
    hada = np.array([[1.0]], np.float32)
    while hada.shape[0] < 128:
        hada = np.block([[hada, hada], [hada, -hada]])
    J = 4
    order = np.arange(arr["L0_attn_w_q_up"].shape[1]).reshape(-1, J, HD).transpose(0, 2, 1).reshape(-1)
    by_row = lambda w: w.reshape(-1, 128, w.shape[1]).transpose(1, 0, 2).reshape(128, -1)
    twice = lambda w: np.concatenate([w, w])
    data = {
        "x_in": arr["L0_attn_x"],
        "first_in": np.concatenate([by_row(arr["L0_c"].T), np.eye(128, dtype=np.float32),
                                    by_row(np.concatenate([arr["L0_attn_w_kv_down"], wrope], axis=1))], axis=1),
        "wmod": arr["L0_wmod"],
        "wq_in": np.concatenate([arr["L0_attn_w_q_down"].T, arr["L0_attn_w_q_up"][:, order]], axis=1),
        "wb_in": np.concatenate([twice(arr["L0_attn_w_kv_up_k"][:, order]), twice(arr["L0_attn_w_kv_up_v"]),
                                 by_row(arr["L0_attn_w_out"])], axis=1),
        "w1t": arr["L0_ffn_W1"].T,
        "w3t": arr["L0_ffn_W3"].T,
        "w2t": arr["L0_ffn_W2"].T,
        "trig_in": np.concatenate([cos, cos, sin, sin]),
        "hada_in": hada,
    }
    nc = bacc.Bacc("TRN2", target_bir_lowering=False, num_devices=1)
    arrays, args = {}, []
    for name, a in data.items():
        a = np.ascontiguousarray(a)
        arrays[name] = a
        args.append(nc.dram_tensor(name, a.shape, mybir.dt.from_np(a.dtype), kind="ExternalInput").ap())
    args.append(nc.dram_tensor("out", data["x_in"].shape, mybir.dt.float32, kind="ExternalOutput").ap())
    adaln_block(nc, *args)
    return run_bass_kernel_spmd(nc, [arrays], core_ids=[0]).results[0]["out"]
```

```python
import concourse.bass as bass
from concourse import mybir
from contextlib import ExitStack


def adaln_block(nc, x_in, first_in, wmod, wq_in, wb_in, w1t, w3t, w2t, trig_in, hada_in, out):
    f32 = mybir.dt.float32
    f32r = mybir.dt.float32r
    ALU = mybir.AluOpType
    ACT = mybir.ActivationFunctionType
    AX = mybir.AxisListType

    P = 128
    B, S, D = x_in.shape
    TT = S // P
    DT = D // P
    HD = trig_in.shape[0] // 4
    HEADS = D // HD
    LAT = P - trig_in.shape[0]
    HID = w1t.shape[1]
    HT = HID // P
    J = 4
    NG = HEADS // J
    STEPS = NG * TT
    LEAD = 6
    PART = 2 * HD
    MROW = 3 * PART
    SCALE = float(1.0 / (2 * HD) ** 0.5)
    EPS = 1e-5
    TILES = J * STEPS
    STACK_DMAS = 3 + 6
    LOADED = 16 * STACK_DMAS
    FW = HT * D // S

    MAXB, SCB, PVB, MISC = 0, 3, 6, 7
    GB, UB, OB = 0, 2, 4

    ctx = ExitStack()
    sem = lambda name: ctx.enter_context(nc.semaphore(name))
    sb = lambda name, shape, dt=f32: ctx.enter_context(nc.sbuf_tensor(name, shape, dt))
    flat = lambda t: t.rearrange("p a s -> p (a s)")

    with ctx:
        ps = ctx.enter_context(nc.psum_tensor("ps", [P, 8, 512], f32))
        inv_dram = nc.dram_tensor("inv_dram", (2 * J, S), f32, kind="Internal").ap()
        gates_dram = nc.dram_tensor("gates_dram", (B, 2 * D), f32, kind="Internal").ap()

        x = sb("x", [P, B, TT, D])
        gate_now = sb("gate_now", [P, D])
        mod_t = sb("mod_t", [P, B, 8])
        stats = sb("stats", [P, TT, 6])
        mean_var = sb("mean_var", [P, TT, 2])
        var_eps, rstd = sb("var_eps", [P, TT]), sb("rstd", [P, TT])
        eps_c, half_c = sb("eps_c", [P, TT]), sb("half_c", [P, TT])
        mod_now = sb("mod_now", [P, 4])
        xn = sb("xn", [P, TT, D])
        h_raw = sb("h_raw", [P, DT, S])
        h_hi, h_lo = sb("h_hi", [P, DT, S], f32r), sb("h_lo", [P, DT, S], f32r)
        Q_LO, Q_HI, K_HI, K_LO = range(4)
        kv = sb("kv", [P, S], f32r)
        trig = sb("trig", [P, S])
        rope_c, rope_s = trig, sb("rope_s", [PART, S])
        r_hi, r_lo = sb("r_hi", [PART, S], f32r), sb("r_lo", [PART, S], f32r)
        v_new = sb("v_new", [P, TT, D])
        maxima = [sb(f"maxima{i}", [P, TT, J]) for i in range(2)]
        neg_max = sb("neg_max", [J, S], f32r)
        pv_sb = sb("pv_sb", [P, S])
        attn, inv = sb("attn", [P, DT, S]), sb("inv", [P, DT, S])
        QS = J * S // P
        sums = sb("sums", [P, 2, QS])
        attn_hi, attn_lo = sb("attn_hi", [P, DT, S], f32r), sb("attn_lo", [P, DT, S], f32r)
        first = sb("first", [P, 2 * B + P + DT * P])
        ct, ident, wkr_raw = (first[:, a:b] for a, b in ((0, 2 * B), (2 * B, 2 * B + P), (2 * B + P, 2 * B + P + DT * P)))
        silu_ct = sb("silu_ct", [P, DT, B])
        wkr_hi, wkr_lo = sb("wkr_hi", [P, DT, P], f32r), sb("wkr_lo", [P, DT, P], f32r)
        wq_hi, wq_lo = sb("wq_hi", [P, DT, D], f32r), sb("wq_lo", [P, DT, D], f32r)
        wb_hi, wb_lo = sb("wb_hi", [P, 4, D], f32r), sb("wb_lo", [P, 4, D], f32r)
        hada = sb("hada", [P, P])

        y_gated = h_raw[:, :, :].rearrange("p a (t d) -> p (a t) d", d=D)
        gate_sign, gate_row = inv[0:B, 0, :], inv[0:B, 1, :]

        def layer(*tensors):
            with ExitStack() as region:
                return [region.enter_context(nc.sbuf_tensor(*tensor)) for tensor in tensors]

        *stack, probs, parts, v_ones = layer(
            *((f"stack{g}", [P, J, 2, S], f32r) for g in range(NG)), ("probs", [P, 2, J, S], f32),
            ("parts", [P, DT, 4, S], f32r), ("v_ones", [P, TT, HEADS, HD, 2], f32))
        w2_raw, w2_mix, w3_hi, w3_lo, w1_hi, w1_lo, w2_hi, w2_lo, hid_hi, w1_raw, w3_raw, silu_sb, hid = layer(
            ("w2_raw", [P, HT, D], f32), ("w2_mix", [P, HT, D], f32),
            ("w3_hi", [P, DT, HID], f32r), ("w3_lo", [P, DT, HID], f32r),
            ("w1_hi", [P, DT, HID], f32r), ("w1_lo", [P, DT, HID], f32r),
            ("w2_hi", [P, HT, D], f32r), ("w2_lo", [P, HT, D], f32r), ("hid_hi", [P, HT, S], f32r),
            ("w1_raw", [P, DT, HID], f32), ("w3_raw", [P, DT, HID], f32),
            ("silu_sb", [P, 2, S], f32), ("hid", [P, 2, S], f32))
        _, wmod_sb, wq_raw, wb_raw, _, hid_lo = layer(
            ("places_0_to_2", [P, (NG - 1) * J * 2 * S], f32), ("wmod_sb", [P, DT, 6 * D + 2 * D], f32),
            ("wq_raw", [P, 2 * D], f32), ("wb_raw", [P, 4 * D], f32), ("rest_of_probs", [P, 2 * J * S - 6 * D], f32),
            ("hid_lo", [P, HT, S], f32r))

        first_in_sb, wmod_a, wmod_b, w_in, trig_in_sb = (sem(n) for n in ("first_in_sb", "wmod_a", "wmod_b", "w_in", "trig_in_sb"))
        x_first, x_second, x_rest = sem("x_first"), sem("x_second"), sem("x_rest")
        silu_c = sem("silu_c")
        mod_psum, mod_sb = sem("mod_psum"), sem("mod_sb")
        wq_psum, w_hi_done, w_lo_done, wq_lo_done = (sem(n) for n in ("wq_psum", "w_hi_done", "w_lo_done", "wq_lo_done"))
        gate_psum, gate_step, gate_sb, gates_sent = (sem(n) for n in ("gate_psum", "gate_step", "gate_sb", "gates_sent"))
        consts, ones_set = sem("consts"), sem("ones_set")
        stats_done, aggr_done, eps_added, rstd_done = (sem(n) for n in ("stats_done", "aggr_done", "eps_added", "rstd_done"))
        centred, xn_done, mod_copied = sem("centred"), sem("xn_done"), sem("mod_copied")
        h_ready, h_hi_done, h_lo_done = sem("h_ready"), sem("h_hi_done"), sem("h_lo_done")
        max_full, max_free = sem("max_full"), sem("max_free")
        sc_full, exp_done = sem("sc_full"), sem("exp_done")
        pv_done, pv_copied, pv_parted = sem("pv_done"), sem("pv_copied"), sem("pv_parted")
        misc_full, tail_full = sem("misc_full"), sem("tail_full")
        kv_hi_done, kv_lo_done = sem("kv_hi_done"), sem("kv_lo_done")
        rope_mul, rope_added = sem("rope_mul"), sem("rope_added")
        rhi_done, rlo_done = sem("rhi_done"), sem("rlo_done")
        hi_done, lo_done = sem("hi_done"), sem("lo_done")
        v_evac, v_ready = sem("v_evac"), sem("v_ready")
        stack_loaded = [sem(f"stack_loaded{g}") for g in range(NG)]
        neg_ready, max_loaded = sem("neg_ready"), sem("max_loaded")
        recip_done, norm_done = sem("recip_done"), sem("norm_done")
        inv_sent, inv_loaded = sem("inv_sent"), sem("inv_loaded")
        attn_hi_done, attn_lo_done = sem("attn_hi_done"), sem("attn_lo_done")
        gate_loaded, y_gated_done, x1_done = sem("gate_loaded"), sem("y_gated_done"), sem("x1_done")
        w_loaded = [sem(f"w_loaded{i}") for i in range(3)]
        w1_split, w3_split, w2_split = sem("w1_split"), sem("w3_split"), sem("w2_split")
        w1_hi_done, w3_hi_done, w2_hi_done = sem("w1_hi_done"), sem("w3_hi_done"), sem("w2_hi_done")
        fw_scaled, fw_stage = sem("fw_scaled"), sem("fw_stage")
        gate_full, up_full, silu_done, hid_done = (sem(n) for n in ("gate_full", "up_full", "silu_done", "hid_done"))
        hid_hi_done, hid_lo_done = sem("hid_hi_done"), sem("hid_lo_done")
        t_full = sem("t_full")
        out_full, out_free, res_done, stored = (sem(n) for n in ("out_full", "out_free", "res_done", "stored"))

        TASKS = [
            (0, "hT0", "ln"), (1, "hT1", "ln"), (2, "maxT1", "cur"), (3, "kvrope", "nxt"),
            (4, "q0", "nxt"), (5, "k0", "nxt"), (6, "maxT2", "cur"), (7, "v0", "nxt"), (7, "fw0", "ffn"),
            (8, "q1", "nxt"), (8, "fw1", "ffn"), (9, "k1", "nxt"), (9, "fw2", "ffn"), (10, "maxT3", "cur"),
            (11, "out0", "prev"), (12, "out1", "prev"), (13, "v1", "nxt"), (13, "fw3", "ffn"),
            (14, "maxT0", "nxt"),
        ]
        FIRST, SECOND = ("ln", "nxt"), ("cur", "ln", "nxt")
        MIDDLE, LAST = ("prev", "cur", "ln", "nxt"), ("prev", "cur", "ln", "ffn")

        class Body:

            def __init__(self, b, kinds, normalised=None):
                self.b, self.kinds = b, kinds
                self.prev, self.cur, self.nxt, self.ffn = (k in kinds for k in ("prev", "cur", "nxt", "ffn"))
                self.normalised = normalised or (b + 2, 0)
                self.tasks = [t for t in TASKS if t[2] in kinds]

            def at(self, step):
                return [t[1] for t in self.tasks if t[0] == step]

            def used(self, name):
                uses = lambda kinds: sum(t[2] in kinds for t in TASKS)
                here = [t[1] for t in self.tasks].index(name)
                if self.kinds == FIRST:
                    return here
                if self.kinds == SECOND:
                    return uses(FIRST) + here
                return self.b * uses(MIDDLE) + (uses(FIRST) + uses(SECOND) - uses(MIDDLE) + here)

        def bank_read(name, n):
            if name == "kvrope":
                return [(kv_lo_done, n + 1), (rope_mul, 2 * n + 2)]
            i = int(name[-1])
            if name[:2] == "fw":
                return [(fw_scaled, i + 1)]
            if name[0] in "qk":
                return [(lo_done, 4 * n + (2 * i + (name[0] == "k") + 1))]
            kind, each = {"hT": (h_ready, DT), "v": (v_evac, 2), "out": (y_gated_done, 2), "maxT": (neg_ready, NG)}[name[:-1]]
            return [(kind, each * n + i + 1)]

        def task_before(k, name):
            sequence = {"prev": k.b - 1, "cur": k.b, "nxt": k.b + 1, "ln": k.b + 1, "ffn": 0}
            here = [(t[1], sequence[t[2]]) for t in k.tasks]
            at = [t[0] for t in here].index(name)
            if at:
                return here[at - 1]
            if k.kinds == FIRST:
                return None
            kinds = {SECOND: FIRST, MIDDLE: SECOND, LAST: MIDDLE}[k.kinds]
            before = [t for t in TASKS if t[2] in kinds][-1]
            return before[1], sequence[before[2]] - 1

        def on(engine, body):
            body(Body(-1, FIRST))
            body(Body(0, SECOND))
            with engine.Fori(1, B - 2) as b:
                body(Body(b, MIDDLE))
            body(Body(B - 2, MIDDLE, (0, 1)))
            body(Body(B - 1, LAST))

        def turns(*backward):
            turn, direction = [0], 1
            for at in range(1, TILES):
                if at in backward:
                    direction = -direction
                turn.append(turn[at - 2] if at in backward else (turn[at - 1] + direction) % 3)
            return turn, [next(d for d in range(1, TILES) if turn[at - d] == turn[at]) for at in range(TILES)]

        long_steps = (3, 11)
        sc_turn, sc_ago = turns(*(J * s + 2 for s in long_steps))
        max_turn, max_ago = turns(*(J * ((s + LEAD) % STEPS) + 3 for s in long_steps))

        def on2(engine, body):
            body(0, True)
            with engine.Fori(1, B - 1) as b:
                body(b, True)
            body(B - 1, False)

        def wait(engine, semaphore, value):
            if not isinstance(value, int) or value > 0:
                engine.wait_ge(semaphore, value)

        def max_at(body, s):
            u = s + LEAD
            if u < STEPS:
                return (body.b, u // TT, u % TT) if body.cur else None
            return (body.b + 1, (u - STEPS) // TT, u % TT) if body.nxt else None

        def terms_of(a, b):
            return ((a[0], b[0]), (a[1], b[0]), (a[0], b[1]))

        transpose_at = lambda first_body: HT - 1 if first_body else 4
        TAIL_OUT_AT = HT - 2
        NORMALISE_AT = [(7, 0), (7, 2), (8, 0), (8, 2), (11, 0)]

        block = ctx.enter_context(nc.Block())

        @block.sync
        def _(sp):
            sp.dma_start(first[:, :], first_in).then_inc(first_in_sb, 16)
            sp.dma_start(x[:, 0, :, :], x_in[0].rearrange("(t p) d -> p t d", p=P)).then_inc(x_first, 16)
            wmod_rows = wmod.rearrange("(t p) n -> p t n", p=P)
            sp.dma_start(wmod_sb[:, :, 0:2 * D], wmod_rows[:, :, 0:2 * D]).then_inc(wmod_a, 16)
            sp.dma_start(wq_raw[:, :], wq_in).then_inc(w_in, 16)
            sp.dma_start(wb_raw[:, :], wb_in).then_inc(w_in, 16)
            sp.dma_start(trig[LAT:P, :], trig_in).then_inc(trig_in_sb, 16)
            sp.dma_start(wmod_sb[:, :, 2 * D:6 * D], wmod_rows[:, :, 2 * D:6 * D]).then_inc(wmod_b, 16)
            sp.dma_start(x[:, 1, :, :], x_in[1].rearrange("(t p) d -> p t d", p=P)).then_inc(x_second, 16)

            def move(to, source, signals):
                sp.dma_start(to.bitcast(f32), source.bitcast(f32)).then_inc(signals, 16)

            def load_stack(n, g, before):
                if g == 0:
                    wait(sp, rlo_done, n + 1)
                if before:
                    wait(sp, sc_full, TILES * (n - 1) + J * TT * (g + 1))
                wait(sp, lo_done, 2 * (2 * n + (g // 2 + 1)))
                rows, t = slice(J * HD * (g % 2), J * HD * (g % 2 + 1)), g // 2
                for part, (one, two) in enumerate(((Q_HI, K_HI), (Q_HI, K_LO), (Q_LO, K_HI))):
                    to = PART * part
                    move(stack[g][to:to + HD, :, :, :].rearrange("p j a s -> p (j a s)"),
                         parts[rows, t, one:two + 1:two - one, :], stack_loaded[g])
                for part, sources in enumerate(((r_hi, r_hi), (r_hi, r_lo), (r_lo, r_hi))):
                    to = PART * part + HD
                    for a, src in enumerate(sources):
                        move(stack[g][to:to + HD, :, a, :],
                             src[a * HD:(a + 1) * HD, :].rearrange("p (o s) -> p o s", o=1).to_broadcast([HD, J, S]),
                             stack_loaded[g])

            def load_max(n, g):
                wait(sp, neg_ready, NG * n + g + 1)
                move(stack[g][MROW:MROW + 1, :, 0, :], neg_max[:, :], max_loaded)

            def part_pv(n, g):
                i, rows = g // 2, slice(J * HD * (g % 2), J * HD * (g % 2 + 1))
                wait(sp, pv_copied, NG * n + g + 1)
                if g == 2:
                    wait(sp, attn_lo_done, DT * n)
                sp.dma_start(attn[rows, i, :], pv_sb[0:P:2, :]).then_inc(pv_parted, 16)
                sp.dma_start(sums[:, g % 2, :], pv_sb[1:P:2 * HD, :]).then_inc(pv_parted, 16)

            def spread_inverses(n, i):
                wait(sp, recip_done, DT * (n + 1) if i else DT * n + 1)
                sp.dma_start(inv_dram.rearrange("(a j) (r q) -> (j r) a q", a=2, q=QS), sums[:, :, :]).then_inc(inv_sent, 16)
                wait(sp, inv_sent, 16 * (DT * n + i + 1))
                sp.dma_start(inv[:, i, :], inv_dram.rearrange("h (o s) -> h o s", o=1)
                             .to_broadcast([2 * J, HD, S])).then_inc(inv_loaded, 16)

            def load_gate(row, which):
                sp.dma_start(gate_now[:, :], gates_dram[row, which * D:(which + 1) * D]
                             .rearrange("(o d) -> o d", o=1).to_broadcast([P, D])).then_inc(gate_loaded, 16)

            def body(k):
                if k.prev:
                    wait(sp, y_gated_done, 2 * (k.b - 1))
                    part_pv(k.b - 1, NG - 1)
                    load_gate(k.b - 1, 0)
                if k.cur:
                    load_stack(k.b, NG - 1, k.prev)
                    load_max(k.b, 1)
                if k.prev:
                    wait(sp, attn_lo_done, DT * (k.b - 1) + 1)
                    spread_inverses(k.b - 1, 1)
                if k.ffn:
                    sp.wait_ge(stack_loaded[NG - 1], LOADED * B)
                    sp.dma_start(w3_raw[:, :, :], w3t.rearrange("(t p) h -> p t h", p=P)).then_inc(w_loaded[1], 16)
                if k.cur:
                    part_pv(k.b, 0)
                if k.ffn:
                    sp.wait_ge(sc_full, TILES * k.b + J * TT)
                    sp.dma_start(w2_raw[:, :, :], w2t.rearrange("(t p) d -> p t d", p=P)).then_inc(w_loaded[2], 16)
                if k.cur:
                    load_max(k.b, 2)
                if k.ffn:
                    sp.dma_start(w1_raw[:, :, :], w1t.rearrange("(t p) h -> p t h", p=P)).then_inc(w_loaded[0], 16)
                if k.nxt:
                    load_stack(k.b + 1, 0, k.cur)
                if k.cur:
                    part_pv(k.b, 1)
                if k.nxt:
                    load_stack(k.b + 1, 1, k.cur)
                if k.cur:
                    load_max(k.b, 3)
                    spread_inverses(k.b, 0)
                if k.nxt:
                    load_stack(k.b + 1, 2, k.cur)
                if k.cur:
                    part_pv(k.b, 2)
                if k.nxt:
                    load_max(k.b + 1, 0)
                if not k.cur:
                    sp.wait_ge(gate_sb, 1)
                    sp.dma_start(gates_dram, gate_row).then_inc(gates_sent, 16)
                    for b in range(2, B):
                        sp.dma_start(x[:, b, :, :], x_in[b].rearrange("(t p) d -> p t d", p=P)).then_inc(x_rest, 16)
                    sp.dma_start(hada[:, :], hada_in).then_inc(x_rest, 16)
                    sp.wait_ge(gates_sent, 16)

            on(sp, body)

            sp.wait_ge(y_gated_done, 2 * (B - 1))
            part_pv(B - 1, NG - 1)
            load_gate(B - 1, 0)
            spread_inverses(B - 1, 1)

            sp.wait_ge(y_gated_done, 2 * B)
            for b in range(B):
                wait(sp, out_free, TT * b)
                load_gate(b, 1)
                pieces = 1 if b < B - 1 else 2
                for i in range(pieces):
                    tiles = slice(i * TT // pieces, (i + 1) * TT // pieces)
                    sp.wait_ge(res_done, TT * b + tiles.stop)
                    sp.dma_start(out[b].rearrange("(t p) d -> p t d", p=P)[:, tiles, :], x[:, b, tiles, :]).then_inc(stored, 16)
            sp.wait_ge(stored, 16 * (B + 1))

        @block.tensor
        def _(pe):
            def modulation(bank, chunks):
                for i, chunk in enumerate(chunks):
                    for t in range(DT):
                        col = chunk * D + t * P
                        for kt in range(DT):
                            last = nc.tensor.matmul(ps[:, bank, (i * DT + t) * B:(i * DT + t + 1) * B],
                                                    wmod_sb[:, kt, col:col + P], silu_ct[:, kt, :],
                                                    start=kt == 0, stop=kt == DT - 1)
                last.then_inc(mod_psum, 1)

            pe.wait_ge(silu_c, 1)
            pe.wait_ge(wmod_a, 16)
            modulation(MISC, (0, 1))

            def query_weights():
                pe.wait_ge(w_in, 32)
                for t in range(DT):
                    last = nc.tensor.matmul(ps[:, PVB, t * D:(t + 1) * D], wq_raw[:, t * P:(t + 1) * P],
                                            wq_raw[:, D:2 * D], start=True, stop=True)
                last.then_inc(wq_psum, 1)

            def later_modulation():
                pe.wait_ge(wmod_b, 16)
                modulation(SCB, (3, 4))

            def raw_gates():
                pe.wait_ge(wmod_b, 16)
                for i, chunk in enumerate((2, 5)):
                    for kt in range(DT):
                        last = nc.tensor.matmul(ps[0:B, SCB + 1, i * D:(i + 1) * D], silu_ct[:, kt, :],
                                                wmod_sb[:, kt, chunk * D:(chunk + 1) * D],
                                                start=kt == 0, stop=kt == DT - 1)
                last.then_inc(gate_psum, 1)

            def product(dst, pairs, n_terms, start=True):
                for i, (a, b) in enumerate(pairs):
                    last = nc.tensor.matmul(dst, a, b, start=start and i == 0, stop=i == n_terms - 1)
                return last

            def transposed(bank, n):
                for t in range(TT):
                    last = nc.tensor.transpose(ps[:, bank, t * P:(t + 1) * P], xn[:, t, n * P:(n + 1) * P], ident)
                return last

            def project_out(bank, n):
                for i in range(2):
                    tokens = slice((2 * n + i) * P, (2 * n + i + 1) * P)
                    pairs = [(a[:, kt, tokens], w[:, 2 + kt, :])
                             for a, w in terms_of((attn_hi, attn_lo), (wb_hi, wb_lo)) for kt in range(DT)]
                    last = product(ps[:, bank, i * D:(i + 1) * D], pairs, len(pairs))
                return last

            def prob_v(b, s):
                pg, pt = divmod(s, TT)
                wait(pe, exp_done, TILES * b + J * (s + 1))
                if pt == 0:
                    wait(pe, v_ready, NG * b + pg + 1)
                    wait(pe, pv_copied, NG * b + pg)
                for j in range(J):
                    last = nc.tensor.matmul(ps[2 * HD * j:2 * HD * (j + 1), PVB, :],
                                            v_ones[:, pt, J * pg + j, :, :].rearrange("p d o -> p (d o)"),
                                            probs[:, s % 2, j, :], start=pt == 0, stop=pt == TT - 1)
                last.then_inc(pv_done, 1)

            def task(k, name):
                bank = MISC
                before = task_before(k, name)
                if before:
                    for semaphore, count in bank_read(*before):
                        wait(pe, semaphore, count)
                n = int(name[-1]) if name[-1].isdigit() else 0
                if name[:2] == "hT":
                    wait(pe, xn_done, 2 * (k.b + 2))
                    last = transposed(bank, n)
                elif name == "kvrope":
                    wait(pe, h_hi_done, DT * (k.b + 2))
                    wait(pe, h_lo_done, DT * (k.b + 2))
                    pairs = [(w[:, t, :], h[:, t, :]) for w, h in terms_of((wkr_hi, wkr_lo), (h_hi, h_lo)) for t in range(DT)]
                    last = product(ps[:, bank, :], pairs, len(pairs))
                elif name[0] == "q":
                    pairs = [(w[:, t, n * P:(n + 1) * P], h[:, t, :])
                             for w, h in terms_of((wq_hi, wq_lo), (h_hi, h_lo)) for t in range(DT)]
                    last = product(ps[:, bank, :], pairs, len(pairs))
                elif name[0] == "k":
                    wait(pe, kv_lo_done, k.b + 2)
                    cols = slice(n * P, (n + 1) * P)
                    last = product(ps[:, bank, :], [(wb_hi[:, 0, cols], kv[:, :]), (wb_lo[0:LAT, 0, cols], kv[0:LAT, :])], 2)
                elif name[0] == "v":
                    for i in range(2):
                        tokens = slice((2 * n + i) * P, (2 * n + i + 1) * P)
                        last = product(ps[:, bank, i * D:(i + 1) * D],
                                       [(kv[:, tokens], wb_hi[:, 1, :]), (kv[0:LAT, tokens], wb_lo[0:LAT, 1, :])], 2)
                elif name[:4] == "maxT":
                    nb = k.b + 1 if n == 0 else k.b
                    wait(pe, max_free, TILES * nb + J * TT * (n + 1))
                    for t in range(TT):
                        last = nc.tensor.transpose(ps[0:J, bank, t * P:(t + 1) * P], maxima[n % 2][:, t, :], ident)
                elif name[:2] == "fw":
                    pe.wait_ge(w_loaded[2], 16)
                    last = nc.tensor.matmul(ps[:, bank, :], hada[:, :], w2_raw[:, :, :].rearrange("p t d -> p (t d)")[:, n * S:(n + 1) * S],
                                            start=True, stop=True)
                else:
                    wait(pe, attn_lo_done, DT * k.b)
                    last = project_out(bank, n)
                last.then_inc(misc_full, 1)

            def body(k):
                if k.kinds == SECOND:
                    pe.wait_ge(ones_set, NG)
                    pe.wait_ge(consts, 2)
                    pe.wait_ge(mod_sb, 4)
                    pe.wait_ge(gate_sb, 1)
                for s in range(STEPS):
                    g, kt = divmod(s, TT)
                    ahead = max_at(k, s)
                    if k.kinds == FIRST and s == 0:
                        pe.wait_ge(mod_sb, 2)
                    if k.kinds == FIRST and s == 2:
                        query_weights()
                    if k.kinds == FIRST and s == 3:
                        pe.wait_ge(w_hi_done, 2)
                        pe.wait_ge(w_lo_done, 2)
                    if k.kinds == FIRST and s == 4:
                        pe.wait_ge(wq_lo_done, 1)
                    if k.kinds == FIRST and s == 6:
                        later_modulation()
                    if k.kinds == FIRST and s == 5:
                        raw_gates()

                    def max_tile(j):
                        n, mg, qt = ahead
                        if qt == 0 and j == 0:
                            wait(pe, stack_loaded[mg], LOADED * (n + 1))
                        at = J * (TT * mg + qt) + j
                        tile = TILES * n + at
                        wait(pe, max_free, tile + (1 - max_ago[at]))
                        nc.tensor.matmul(ps[:, MAXB + max_turn[at], :], stack[mg][0:MROW, j, 0, qt * P:(qt + 1) * P],
                                         stack[mg][0:MROW, j, 1, :], start=True, stop=True).then_inc(max_full, 1)

                    def score_tile(j):
                        if kt == 0 and j == 0:
                            wait(pe, max_loaded, 16 * (NG * k.b + g + 1))
                        at = J * s + j
                        wait(pe, exp_done, TILES * k.b + (at + 1 - sc_ago[at]))
                        nc.tensor.matmul(ps[:, SCB + sc_turn[at], :], stack[g][0:MROW + 1, j, 1, kt * P:(kt + 1) * P],
                                         stack[g][0:MROW + 1, j, 0, :], start=True, stop=True).then_inc(sc_full, 1)

                    for j, tile in ((0, max_tile), (0, score_tile), (1, max_tile), (1, score_tile), (2, max_tile),
                                    (2, score_tile), (3, max_tile), (3, score_tile)):
                        if (j, tile) == (2, score_tile):
                            for name in k.at(s):
                                task(k, name)
                            if s > 0 and k.cur:
                                prob_v(k.b, s - 1)
                            if s == 0 and k.prev:
                                prob_v(k.b - 1, STEPS - 1)
                        if ahead if tile is max_tile else k.cur:
                            tile(j)

            on(pe, body)

            def body2(b, nxt):
                n = b + B
                wait(pe, h_hi_done, DT * (n + 1))
                wait(pe, h_lo_done, DT * (n + 1))
                first_body = isinstance(b, int) and b == 0
                for m in range(HT):
                    cols = slice(m * P, (m + 1) * P)
                    for bank, full, read, (w_hi, w_lo), split in (
                            (GB, gate_full, silu_done, (w1_hi, w1_lo), w1_split),
                            (UB, up_full, hid_done, (w3_hi, w3_lo), w3_split)):
                        if first_body and m == 0:
                            pe.wait_ge(split, DT)
                        wait(pe, read, HT * b + m - 1)
                        pairs = [(w[:, kt, cols], h[:, kt, :])
                                 for w, h in terms_of((w_hi, w_lo), (h_hi, h_lo)) for kt in range(DT)]
                        product(ps[:, bank + m % 2, :], pairs, len(pairs)).then_inc(full, 1)
                        if first_body and m == 0 and bank == GB:
                            prob_v(B - 1, STEPS - 1)
                    if first_body and m == TAIL_OUT_AT:
                        pe.wait_ge(attn_lo_done, DT * B)
                        pe.wait_ge(neg_ready, NG * B)
                        pe.wait_ge(fw_scaled, FW)
                        pe.wait_ge(pv_copied, NG * B)
                        for i, bank in enumerate((MISC, PVB)):
                            project_out(bank, i).then_inc(tail_full, 1)
                    if m == transpose_at(first_body) and nxt:
                        wait(pe, out_free, TT * b)
                        wait(pe, xn_done, 2 * (n + 2))
                        for t2 in range(DT):
                            transposed(OB + t2, t2).then_inc(t_full, 1)
                if first_body:
                    pe.wait_ge(y_gated_done, 2 * B)
                    pe.wait_ge(w2_split, DT)
                wait(pe, h_ready, DT * (n + 2) if nxt else DT * (n + 1))
                wait(pe, out_free, TT * b)
                for m in range(HT):
                    wait(pe, hid_hi_done, HT * b + m + 1)
                    wait(pe, hid_lo_done, HT * b + m + 1)
                    for t in range(TT):
                        rows = slice(t * P, (t + 1) * P)
                        for i, (h, w) in enumerate(terms_of((hid_hi, hid_lo), (w2_hi, w2_lo))):
                            last = nc.tensor.matmul(ps[:, OB + t, 0:D], h[:, m, rows], w[:, m, :],
                                                    start=m == 0 and i == 0, stop=m == HT - 1 and i == 2)
                        if m == HT - 1:
                            last.then_inc(out_full, 1)

            on2(pe, body2)

        @block.scalar
        def _(act):
            act.wait_ge(first_in_sb, 16)
            nc.scalar.activation(silu_ct[:, :, :].rearrange("p t b -> p (t b)"), ct, ACT.Silu).then_inc(silu_c, 1)
            nc.scalar.copy(flat(wkr_hi[:, :, :]), wkr_raw).then_inc(w_hi_done, 1)
            act.wait_ge(w_in, 32)
            nc.scalar.copy(flat(wb_hi[:, :, :]), wb_raw[:, :]).then_inc(w_hi_done, 1)

            def modulate(n, i, bank):
                if i == 0:
                    wait(act, mod_copied, n + 1)
                nc.scalar.activation(h_raw[:, i, :], ps[:, bank, :], ACT.Identity,
                                     scale=mod_now[:, 2 + i:3 + i], bias=mod_now[:, i:i + 1]).then_inc(h_ready, 1)

            def h_hi_part(n, i):
                wait(act, h_ready, DT * n + i + 1)
                nc.scalar.copy(h_hi[:, i, :], h_raw[:, i, :]).then_inc(h_hi_done, 1)

            def copy_pv(n, g):
                wait(act, pv_done, STEPS * n + TT * (g + 1))
                wait(act, pv_parted, 32 * (NG * n + g))
                nc.scalar.copy(pv_sb[:, :], ps[:, PVB, :]).then_inc(pv_copied, 1)

            def attn_hi_part(n, i):
                wait(act, norm_done, DT * n + i + 1)
                wait(act, y_gated_done, 2 * n)
                nc.scalar.copy(attn_hi[:, i, :], attn[:, i, :]).then_inc(attn_hi_done, 1)

            def body(k):
                for s in range(STEPS):
                    if k.kinds == FIRST and s == 3:
                        act.wait_ge(wq_psum, 1)
                        nc.scalar.copy(flat(wq_hi[:, :, :]), ps[:, PVB, :]).then_inc(w_hi_done, 1)
                    for j in range(J):
                        if s % TT == 0 and j == J - 1:
                            if s == 0 and k.prev:
                                copy_pv(k.b - 1, NG - 1)
                            elif s and k.cur:
                                copy_pv(k.b, s // TT - 1)
                        if (s, j) == (7, 0) and k.prev:
                            attn_hi_part(k.b - 1, 1)
                        if (s, j) == (15, 2) and k.cur:
                            attn_hi_part(k.b, 0)
                        if j == J // 2:
                            for name in k.at(s):
                                read_task(k, name)
                        if k.cur:
                            exponentials(k, s, j)

            def exponentials(k, s, j):
                wait(act, sc_full, TILES * k.b + J * s + j + 1)
                if j == 0:
                    wait(act, pv_done, STEPS * k.b + s - 1)
                nc.scalar.activation(probs[:, s % 2, j, :], ps[:, SCB + sc_turn[J * s + j], :], ACT.Exp, scale=SCALE).then_inc(exp_done, 1)

            def read_task(k, name):
                bank = MISC
                n = int(name[-1]) if name[-1].isdigit() else 0
                if name[:2] == "hT":
                    if n == 0:
                        wait(act, x1_done, 2 * (k.b - 1))
                        wait(act, h_lo_done, DT * (k.b + 1))
                        wait(act, lo_done, 4 * (k.b + 1))
                    wait(act, misc_full, k.used(name) + 1)
                    modulate(k.b + 1, n, bank)
                elif name == "kvrope":
                    wait(act, v_evac, 2 * (k.b + 1))
                    wait(act, misc_full, k.used(name) + 1)
                    nc.scalar.copy(kv[0:LAT, :], ps[0:LAT, bank, :]).then_inc(kv_hi_done, 1)
                elif name[0] in "qk":
                    wait(act, stack_loaded[2 * n + 1], LOADED * (k.b + 1))
                    wait(act, misc_full, k.used(name) + 1)
                    nc.scalar.copy(parts[:, n, Q_HI if name[0] == "q" else K_HI, :], ps[:, bank, :]).then_inc(hi_done, 1)
                elif name[0] == "v":
                    wait(act, v_ready, NG * (k.b + 1))
                    wait(act, misc_full, k.used(name) + 1)
                    nc.scalar.copy(v_new[:, 2 * n:2 * n + 2, :], ps[:, bank, :].rearrange("p (t d) -> p t d", t=2)).then_inc(v_evac, 1)
                elif name[:4] == "maxT":
                    nb = k.b + 1 if n == 0 else k.b
                    wait(act, max_loaded, 16 * (NG * nb + n))
                    wait(act, misc_full, k.used(name) + 1)
                    nc.scalar.activation(neg_max[:, :], ps[0:J, bank, :], ACT.Copy, scale=-1.0).then_inc(neg_ready, 1)
                elif name[:2] == "fw":
                    wait(act, misc_full, k.used(name) + 1)
                    nc.scalar.activation(w2_mix[:, :, :].rearrange("p t d -> p (t d)")[:, n * S:(n + 1) * S],
                                         ps[:, bank, :], ACT.Copy, scale=float(HID ** -0.5)).then_inc(fw_scaled, 1)

            on(act, body)

            copy_pv(B - 1, NG - 1)

            def body2(b, nxt):
                first_body = isinstance(b, int) and b == 0
                for m in range(HT + 1):
                    if m < HT:
                        wait(act, gate_full, HT * b + m + 1)
                        wait(act, hid_done, HT * b + m - 1)
                        nc.scalar.activation(silu_sb[:, m % 2, :], ps[:, GB + m % 2, :], ACT.Silu).then_inc(silu_done, 1)
                    if m >= 1:
                        wait(act, hid_done, HT * b + m)
                        nc.scalar.copy(hid_hi[:, m - 1, :], hid[:, (m - 1) % 2, :]).then_inc(hid_hi_done, 1)
                    if first_body and m == 4:
                        attn_hi_part(B - 1, 1)
                    if first_body and m in (1, 2):
                        half = slice((m - 1) * HT // 2, m * HT // 2)
                        act.wait_ge(fw_stage, 6)
                        nc.scalar.copy(w2_hi[:, half, :], w2_raw[:, half, :]).then_inc(w2_hi_done, 1)
                    if m == transpose_at(first_body) + 1 and nxt:
                        n = b + (B + 1)
                        if first_body:
                            act.wait_ge(x1_done, 2 * B)
                        else:
                            act.wait_ge(res_done, TT * b)
                        for i in range(DT):
                            wait(act, t_full, DT * b + i + 1)
                            modulate(n, i, OB + i)
                if nxt:
                    n = b + (B + 1)
                    wait(act, up_full, HT * b + HT)
                    for i in range(DT):
                        h_hi_part(n, i)
            on2(act, body2)

        @block.vector
        def _(dve):
            def statistics(n, at, t):
                nc.vector.bn_stats(stats[:, t, :], x[:, at, t, :]).then_inc(stats_done, 1)

            def aggregates(n, n_mod=None):
                wait(dve, stats_done, TT * (n + 1))
                if n_mod is not None:
                    at, part = n_mod
                    nc.vector.tensor_copy(mod_now[:, :], mod_t[:, at, 4 * part:4 * part + 4]).then_inc(mod_copied, 1)
                for t in range(TT):
                    nc.vector.bn_aggr(mean_var[:, t, :], stats[:, t, :]).then_inc(aggr_done, 1)

            nc.vector.memset(eps_c[:, :], EPS)
            nc.vector.memset(half_c[:, :], -0.5).then_inc(consts, 1)
            for g in range(2):
                nc.vector.memset(stack[g][MROW:MROW + 1, :, 1, :].bitcast(f32), 1.0).then_inc(ones_set, 1)
            dve.wait_ge(x_first, 16)
            for t in range(TT):
                statistics(0, 0, t)
            aggregates(0)

            def modulation(half, bank):
                dve.wait_ge(mod_psum, half + 1)
                modp = ps[:, bank, 0:4 * B].rearrange("p (i b) -> p b i", b=B)
                for i in range(2):
                    nc.vector.tensor_scalar(mod_t[:, :, 4 * half + 2 * i:4 * half + 2 * i + 2], modp[:, :, 2 * i:2 * i + 2],
                                            float(i), None, ALU.add).then_inc(mod_sb, 1)

            dve.wait_ge(rstd_done, 1)
            for t in range(TT):
                last = nc.vector.tensor_scalar(xn[:, t, :], x[:, 0, t, :], mean_var[:, t, 0:1],
                                               rstd[:, t:t + 1], ALU.subtract, ALU.mult)
                if t % 2:
                    last.then_inc(xn_done, 1)
            modulation(0, MISC)
            dve.wait_ge(mod_sb, 2)
            nc.vector.tensor_copy(mod_now[:, :], mod_t[:, 0, 0:4]).then_inc(mod_copied, 1)

            nc.vector.memset(stack[2][MROW:MROW + 1, :, 1, :].bitcast(f32), 1.0).then_inc(ones_set, 1)

            def guarded_gates():
                dve.wait_ge(gate_psum, 1)
                gate_in = ps[0:B, SCB + 1, :]
                nc.vector.tensor_scalar(gate_sign, gate_in, 0.0, 2.0, ALU.is_ge, ALU.mult).then_inc(gate_step, 1)
                dve.wait_ge(gate_step, 1)
                nc.vector.tensor_scalar(gate_sign, gate_sign, -1.0, None, ALU.add).then_inc(gate_step, 1)
                dve.wait_ge(gate_step, 2)
                nc.vector.tensor_tensor(gate_row, gate_in, gate_sign, ALU.mult).then_inc(gate_step, 1)
                dve.wait_ge(gate_step, 3)
                nc.vector.scalar_tensor_tensor(out=gate_row, in0=gate_row, scalar=0.25, in1=gate_sign,
                                               op0=ALU.max, op1=ALU.mult).then_inc(gate_sb, 1)

            def layer_norm(n, at, part, t):
                if t < TT:
                    if t == 0:
                        wait(dve, h_ready, DT * n)
                    statistics(n, at, t)
                else:
                    aggregates(n, (at, part))

            def invert_sums(n, i):
                wait(dve, pv_parted, 32 * (NG * n + 2 * i + 2))
                nc.vector.reciprocal(sums[:, :, :], sums[:, :, :]).then_inc(recip_done, 1)

            def normalise_attn(n, i):
                wait(dve, inv_loaded, 16 * (DT * n + i + 1))
                nc.vector.tensor_tensor(attn[:, i, :], attn[:, i, :], inv[:, i, :], ALU.mult).then_inc(norm_done, 1)

            def gate_attn(n, i, bank):
                if i == 0:
                    wait(dve, gate_loaded, 16 * (n + 1))
                ga = gate_now[:, :].rearrange("p (o d) -> p o d", o=1).to_broadcast([P, 2, D])
                nc.vector.tensor_tensor(y_gated[:, 2 * i:2 * i + 2, :], ps[:, bank, :].rearrange("p (t d) -> p t d", t=2),
                                        ga, ALU.mult).then_inc(y_gated_done, 1)

            def butterfly(stage):
                h = 1 << stage
                src, dst = (w2_mix, w2_raw) if stage % 2 == 0 else (w2_raw, w2_mix)
                a, c = (v[:, :, :].rearrange("p (n two h) d -> p n two (h d)", two=2, h=h) for v in (src, dst))
                dve.wait_ge(*((fw_stage, 2 * stage) if stage else (fw_scaled, FW)))
                nc.vector.tensor_tensor(c[:, :, 0, :], a[:, :, 0, :], a[:, :, 1, :], ALU.add).then_inc(fw_stage, 1)
                nc.vector.tensor_tensor(c[:, :, 1, :], a[:, :, 0, :], a[:, :, 1, :], ALU.subtract).then_inc(fw_stage, 1)

            def body(k):
                for s in range(STEPS):
                    if k.kinds == FIRST and s == 3:
                        dve.wait_ge(w_hi_done, 3)
                        nc.vector.tensor_tensor(flat(wq_lo[:, :, :]), ps[:, PVB, :], flat(wq_hi[:, :, :]).bitcast(f32), ALU.subtract).then_inc(wq_lo_done, 1)
                    if k.kinds == FIRST and s == 7:
                        modulation(1, SCB)
                        guarded_gates()
                    for j in range(J):
                        if j == J - 1:
                            for name in k.at(s):
                                read_task(k, name)
                        if s in (1, 2) and j == 0:
                            h_hi_part(k.b + 1, s - 1)
                        if max_at(k, s):
                            reduce_max(*max_at(k, s), j)
                        if k.nxt and (s, j) in NORMALISE_AT:
                            t = NORMALISE_AT.index((s, j))
                            if t == 0 and k.kinds == FIRST:
                                dve.wait_ge(x_second, 16)
                            if t == 0 and k.kinds == SECOND:
                                dve.wait_ge(x_rest, 16 * (B - 1))
                            layer_norm(k.b + 2, *k.normalised, t)
                        if (s, j) == (2, 0) and k.prev:
                            invert_sums(k.b - 1, 1)
                        if (s, j) == (6, 3) and k.prev:
                            normalise_attn(k.b - 1, 1)
                        if (s, j) == (11, 2) and k.cur:
                            invert_sums(k.b, 0)
                        if (s, j) == (13, 1) and k.cur:
                            normalise_attn(k.b, 0)
                    if k.ffn and s in (10, 11):
                        if s == 10:
                            dve.wait_ge(sc_full, TILES * k.b + J * TT * 2)
                            dve.wait_ge(w_loaded[1], 16)
                        nc.vector.tensor_copy(w3_hi[:, s - 10, :], w3_raw[:, s - 10, :]).then_inc(w3_hi_done, 1)
                    if k.ffn and s in (14, 15):
                        butterfly(s - 14)
                    if k.ffn and s in (12, 13):
                        if s == 12:
                            dve.wait_ge(sc_full, TILES * k.b + J * TT * 3)
                            dve.wait_ge(w_loaded[0], 16)
                        nc.vector.tensor_copy(w1_hi[:, s - 12, :], w1_raw[:, s - 12, :]).then_inc(w1_hi_done, 1)
                        dve.wait_ge(w1_hi_done, s - 11)
                        nc.vector.tensor_tensor(w1_lo[:, s - 12, :], w1_raw[:, s - 12, :], w1_hi[:, s - 12, :].bitcast(f32), ALU.subtract).then_inc(w1_split, 1)

            def h_hi_part(n, i):
                wait(dve, h_ready, DT * n + i + 1)
                nc.vector.tensor_copy(h_hi[:, i, :], h_raw[:, i, :]).then_inc(h_hi_done, 1)

            def reduce_max(n, mg, qt, j):
                at = J * (TT * mg + qt) + j
                wait(dve, max_full, TILES * n + at + 1)
                nc.vector.tensor_reduce(out=maxima[mg % 2][:, qt, j:j + 1], in_=ps[:, MAXB + max_turn[at], :],
                                        axis=AX.X, op=ALU.max).then_inc(max_free, 1)

            def read_task(k, name):
                bank = MISC
                n = int(name[-1]) if name[-1].isdigit() else 0
                if name == "kvrope":
                    wait(dve, rlo_done, k.b + 1)
                    wait(dve, misc_full, k.used(name) + 1)
                    if k.kinds == FIRST:
                        dve.wait_ge(trig_in_sb, 16)
                    nc.vector.tensor_tensor(rope_c[0:PART, :], ps[LAT:LAT + PART, bank, :], trig[LAT:LAT + PART, :], ALU.mult).then_inc(rope_mul, 1)
                    wait(dve, kv_hi_done, k.b + 2)
                    nc.vector.tensor_tensor(kv[LAT:P, :], ps[0:LAT, bank, :], kv[0:LAT, :].bitcast(f32), ALU.subtract).then_inc(kv_lo_done, 1)
                    nc.vector.tensor_tensor(rope_s[:, :], ps[LAT + PART:P, bank, :], trig[LAT + PART:P, :], ALU.mult).then_inc(rope_mul, 1)
                elif name[:3] == "out":
                    wait(dve, misc_full, k.used(name) + 1)
                    if n == 0:
                        wait(dve, h_lo_done, DT * (k.b + 2))
                    gate_attn(k.b - 1, n, bank)
                elif name[0] in "qk":
                    order = 2 * n + (name[0] == "k")
                    hi, lo = (parts[:, n, i, :] for i in ((Q_HI, Q_LO) if name[0] == "q" else (K_HI, K_LO)))
                    wait(dve, stack_loaded[2 * n + 1], LOADED * (k.b + 1))
                    wait(dve, hi_done, 4 * (k.b + 1) + order + 1)
                    nc.vector.tensor_tensor(lo, ps[:, bank, :], hi.bitcast(f32), ALU.subtract).then_inc(lo_done, 1)

            on(dve, body)

            def body2(b, nxt):
                first_body = isinstance(b, int) and b == 0
                for m in range(HT + 1):
                    if first_body and m == TAIL_OUT_AT + 1:
                        for i, bank in enumerate((MISC, PVB)):
                            dve.wait_ge(tail_full, i + 1)
                            gate_attn(B - 1, i, bank)
                    if m < HT:
                        wait(dve, silu_done, HT * b + m + 1)
                        wait(dve, up_full, HT * b + m + 1)
                        wait(dve, hid_lo_done, HT * b + m - 1)
                        nc.vector.tensor_tensor(hid[:, m % 2, :], ps[:, UB + m % 2, :], silu_sb[:, m % 2, :], ALU.mult).then_inc(hid_done, 1)
                    if m >= 1:
                        wait(dve, hid_hi_done, HT * b + m)
                        nc.vector.tensor_tensor(hid_lo[:, m - 1, :], hid[:, (m - 1) % 2, :],
                                                hid_hi[:, m - 1, :].bitcast(f32), ALU.subtract).then_inc(hid_lo_done, 1)
                    if first_body and m == 0:
                        butterfly(2)
                    if first_body and m == 1:
                        invert_sums(B - 1, 1)
                    if first_body and m == 3:
                        normalise_attn(B - 1, 1)
                    if first_body and m == 4:
                        dve.wait_ge(w2_hi_done, 2)
                        half = slice(HT // 2, HT)
                        nc.vector.tensor_tensor(w2_lo[:, half, :], w2_raw[:, half, :], w2_hi[:, half, :].bitcast(f32), ALU.subtract).then_inc(w2_split, 1)
                    if nxt and m == 0:
                        if not first_body:
                            dve.wait_ge(x1_done, 2 * B)
                        for t in range(TT + 1):
                            layer_norm(b + (B + 1), b + 1, 1, t)
                for t in range(TT):
                    wait(dve, out_full, TT * b + t + 1)
                    if t == 0:
                        wait(dve, res_done, TT * b)
                        wait(dve, gate_loaded, 16 * (B + b + 1))
                        if nxt:
                            wait(dve, h_lo_done, DT * (b + (B + 2)))
                    nc.vector.tensor_tensor(y_gated[:, t, :], ps[:, OB + t, 0:D], gate_now[:, :], ALU.mult).then_inc(out_free, 1)
            on2(dve, body2)

        @block.gpsimd
        def _(pool):
            nc.gpsimd.memset(v_ones[:, :, :, :, :], 1.0).then_inc(consts, 1)
            pool.wait_ge(consts, 2)

            def deviation(n):
                wait(pool, aggr_done, TT * (n + 1))
                wait(pool, xn_done, 2 * n)
                nc.gpsimd.tensor_tensor(var_eps[:, :], mean_var[:, :, 1], eps_c[:, :], ALU.add).then_inc(eps_added, 1)
                wait(pool, eps_added, n + 1)
                nc.gpsimd.tensor_tensor(rstd[:, :], var_eps[:, :], half_c[:, :], ALU.pow).then_inc(rstd_done, 1)

            def normalise(n, at):
                wait(pool, rstd_done, n + 1)
                for i in range(2):
                    tiles = slice(2 * i, 2 * i + 2)
                    nc.gpsimd.tensor_tensor(xn[:, tiles, :], x[:, at, tiles, :],
                                            mean_var[:, tiles, 0:1].to_broadcast([P, 2, D]), ALU.subtract).then_inc(centred, 1)
                    wait(pool, centred, 2 * (n - 1) + (i + 1))
                    nc.gpsimd.tensor_tensor(xn[:, tiles, :], xn[:, tiles, :],
                                            rstd[:, tiles].rearrange("p (t o) -> p t o", o=1).to_broadcast([P, 2, D]), ALU.mult).then_inc(xn_done, 1)

            def h_lo_parts(n):
                for i in range(DT):
                    wait(pool, h_hi_done, DT * n + i + 1)
                    nc.gpsimd.tensor_tensor(h_lo[:, i, :], h_raw[:, i, :], h_hi[:, i, :].bitcast(f32), ALU.subtract).then_inc(h_lo_done, 1)

            def attn_lo_part(n, i):
                wait(pool, attn_hi_done, DT * n + i + 1)
                wait(pool, y_gated_done, 2 * n)
                nc.gpsimd.tensor_tensor(attn_lo[:, i, :], attn[:, i, :], attn_hi[:, i, :].bitcast(f32), ALU.subtract).then_inc(attn_lo_done, 1)

            def add_attention(n, i):
                wait(pool, y_gated_done, 2 * n + i + 1)
                here = x[:, n, 2 * i:2 * i + 2, :]
                nc.gpsimd.tensor_tensor(here, here, y_gated[:, 2 * i:2 * i + 2, :], ALU.add).then_inc(x1_done, 1)

            deviation(0)
            for i, (lo, raw, hi) in enumerate(((wkr_lo, wkr_raw, wkr_hi), (wb_lo, wb_raw[:, :], wb_hi))):
                pool.wait_ge(w_hi_done, i + 1)
                nc.gpsimd.tensor_tensor(flat(lo[:, :, :]), raw, flat(hi[:, :, :]).bitcast(f32), ALU.subtract).then_inc(w_lo_done, 1)

            def copy_v(n, g, waits):
                wait(pool, v_evac, 2 * (n + 1))
                if waits:
                    wait(pool, pv_done, STEPS * (n - 1) + TT * (g + 1))
                new = v_new[:, :, J * HD * g:J * HD * (g + 1)].rearrange("p t (j d) -> p t j d", j=J)
                place = v_ones[:, :, J * g:J * (g + 1), :, :]
                nc.gpsimd.tensor_tensor(place[:, :, :, :, 0], new, place[:, :, :, :, 1], ALU.mult).then_inc(v_ready, 1)

            def body(k):
                if k.cur:
                    copy_v(k.b, NG - 1, k.prev)
                h_lo_parts(k.b + 1)
                if k.nxt:
                    wait(pool, stack_loaded[NG - 1], LOADED * (k.b + 1))
                    wait(pool, rope_mul, 2 * (k.b + 2))
                    turned = rope_c[0:PART, :]
                    nc.gpsimd.tensor_tensor(r_hi[:, :], turned, rope_s[:, :], ALU.add).then_inc(rhi_done, 1)
                    wait(pool, rhi_done, k.b + 2)
                    nc.gpsimd.tensor_tensor(turned, turned, rope_s[:, :], ALU.add).then_inc(rope_added, 1)
                    wait(pool, rope_added, k.b + 2)
                    nc.gpsimd.tensor_tensor(r_lo[:, :], turned, r_hi[:, :].bitcast(f32), ALU.subtract).then_inc(rlo_done, 1)
                if k.kinds == FIRST:
                    pool.wait_ge(rlo_done, 1)
                    pool.wait_ge(mod_psum, 2)
                    nc.gpsimd.memset(stack[NG - 1][MROW:MROW + 1, :, 1, :].bitcast(f32), 1.0).then_inc(ones_set, 1)
                    pool.wait_ge(ones_set, NG)
                if k.prev:
                    attn_lo_part(k.b - 1, 1)
                if k.nxt:
                    deviation(k.b + 2)
                    normalise(k.b + 2, k.normalised[0])
                if k.ffn:
                    for i in range(DT):
                        pool.wait_ge(w3_hi_done, i + 1)
                        nc.gpsimd.tensor_tensor(w3_lo[:, i, :], w3_raw[:, i, :], w3_hi[:, i, :].bitcast(f32), ALU.subtract).then_inc(w3_split, 1)
                if k.prev:
                    for i in range(2):
                        add_attention(k.b - 1, i)
                if k.nxt:
                    for g in range(NG - 1):
                        copy_v(k.b + 1, g, k.cur)
                if k.cur:
                    attn_lo_part(k.b, 0)

            on(pool, body)

            def body2(b, nxt):
                first_body = isinstance(b, int) and b == 0
                n = b + (B + 1)
                if nxt:
                    deviation(n)
                    normalise(n, b + 1)
                if first_body:
                    attn_lo_part(B - 1, 1)
                    pool.wait_ge(w2_hi_done, 1)
                    half = slice(0, HT // 2)
                    nc.gpsimd.tensor_tensor(w2_lo[:, half, :], w2_raw[:, half, :], w2_hi[:, half, :].bitcast(f32), ALU.subtract).then_inc(w2_split, 1)
                    for i in range(2):
                        add_attention(B - 1, i)
                if nxt:
                    wait(pool, up_full, HT * b + HT)
                    h_lo_parts(n)
                for t in range(TT):
                    wait(pool, out_free, TT * b + t + 1)
                    here = x[:, b, t, :]
                    nc.gpsimd.tensor_tensor(here, here, y_gated[:, t, :], ALU.add).then_inc(res_done, 1)
            on2(pool, body2)


def kernel(**inputs):
    import numpy as np
    import concourse.bacc as bacc
    from concourse.bass_utils import run_bass_kernel_spmd

    arr = {n: np.ascontiguousarray(v) for n, v in inputs.items()}
    S, HD = arr["L0_attn_x"].shape[1], arr["L0_attn_w_k_rope"].shape[1]
    swap = np.arange(HD) ^ 1
    wq_r, wk_r = arr["L0_attn_w_q_rope"], arr["L0_attn_w_k_rope"]
    wrope = np.concatenate([wq_r, wk_r, wq_r[:, swap], wk_r[:, swap]], axis=1)
    inv_freq = (1.0 / np.float32(10000.0) ** (np.arange(0, HD, 2, dtype=np.float32) / np.float32(HD))).astype(np.float32)
    ang = inv_freq[:, None] * np.arange(S, dtype=np.float32)[None, :]
    cos = np.repeat(np.cos(ang).astype(np.float32), 2, axis=0)
    sign = np.tile(np.array([-1.0, 1.0], np.float32), HD // 2)[:, None]
    sin = np.repeat(np.sin(ang).astype(np.float32), 2, axis=0) * sign
    hada = np.array([[1.0]], np.float32)
    while hada.shape[0] < 128:
        hada = np.block([[hada, hada], [hada, -hada]])
    J = 4
    order = np.arange(arr["L0_attn_w_q_up"].shape[1]).reshape(-1, J, HD).transpose(0, 2, 1).reshape(-1)
    by_row = lambda w: w.reshape(-1, 128, w.shape[1]).transpose(1, 0, 2).reshape(128, -1)
    twice = lambda w: np.concatenate([w, w])
    data = {
        "x_in": arr["L0_attn_x"],
        "first_in": np.concatenate([by_row(arr["L0_c"].T), np.eye(128, dtype=np.float32),
                                    by_row(np.concatenate([arr["L0_attn_w_kv_down"], wrope], axis=1))], axis=1),
        "wmod": arr["L0_wmod"],
        "wq_in": np.concatenate([arr["L0_attn_w_q_down"].T, arr["L0_attn_w_q_up"][:, order]], axis=1),
        "wb_in": np.concatenate([twice(arr["L0_attn_w_kv_up_k"][:, order]), twice(arr["L0_attn_w_kv_up_v"]),
                                 by_row(arr["L0_attn_w_out"])], axis=1),
        "w1t": arr["L0_ffn_W1"].T,
        "w3t": arr["L0_ffn_W3"].T,
        "w2t": arr["L0_ffn_W2"].T,
        "trig_in": np.concatenate([cos, cos, sin, sin]),
        "hada_in": hada,
    }
    nc = bacc.Bacc("TRN2", target_bir_lowering=False, num_devices=1)
    arrays, args = {}, []
    for name, a in data.items():
        a = np.ascontiguousarray(a)
        arrays[name] = a
        args.append(nc.dram_tensor(name, a.shape, mybir.dt.from_np(a.dtype), kind="ExternalInput").ap())
    args.append(nc.dram_tensor("out", data["x_in"].shape, mybir.dt.float32, kind="ExternalOutput").ap())
    adaln_block(nc, *args)
    return run_bass_kernel_spmd(nc, [arrays], core_ids=[0]).results[0]["out"]
```
